# Optimizing a Trainium2 kernel written in Bass

```python
import numpy as np
import jax
import jax.numpy as jnp

def _softmax(x, axis=-1):
    return jax.nn.softmax(x, axis=axis)

def _gelu(x):
    return jax.nn.gelu(x, approximate=True)

def _silu(x):
    return jax.nn.silu(x)

def _sigmoid(x):
    return jax.nn.sigmoid(x)

def _layernorm(x, axis=-1, eps=1e-05):
    m = jnp.mean(x, axis=axis, keepdims=True)
    v = jnp.var(x, axis=axis, keepdims=True)
    return (x - m) / jnp.sqrt(v + eps)

def _scatter_add(tgt, idx, src, axis=0):
    return tgt.at[idx].add(src)

def _segment_sum(src, seg, n):
    return jax.ops.segment_sum(src, seg, n)
kernel_name = 'mk_flamingo_gated_d1_seqx_r4_3d1d4a'

def setup_inputs(seed: int=0):
    np.random.seed(seed)
    _w = jnp.asarray

    def _rec_inputs():
        import jax
        import jax.numpy as jnp
        _rk = jax.random.key(seed)
        x = -0.0002928 + 1 * jax.random.normal(jax.random.fold_in(_rk, 1), (8, 512, 256), jnp.float32)
        _lenS = 512 - jax.random.randint(jax.random.fold_in(_rk, 7), (8,), 0, max(1, 512 // 4) + 1, jnp.int32)
        _lenS2 = 512 - jax.random.randint(jax.random.fold_in(_rk, 8), (8,), 0, max(1, 512 // 4) + 1, jnp.int32)
        _ctx_1024P = jax.random.normal(jax.random.fold_in(_rk, 11), (8, 16, 256), jnp.float32)
        _ctx_1024c = jax.random.dirichlet(jax.random.fold_in(_rk, 511), 0.3 * jnp.ones((16,), jnp.float32), (8, 512))
        _ctx_1024t = jnp.einsum('bsk,bkd->bsd', _ctx_1024c, _ctx_1024P)
        _ctx_1024t = _ctx_1024t * jax.lax.rsqrt(jnp.mean(jnp.square(_ctx_1024t)) + 1e-12) * 0.953939
        ctx_1024 = -1.39393e-06 + 0.999914 * (_ctx_1024t + 0.3 * jax.random.normal(jax.random.fold_in(_rk, 611), (8, 512, 256), jnp.float32))
        _g = jax.random.normal(jax.random.fold_in(_rk, 9001), (2, 1), jnp.float32)
        _g = jnp.sign(_g) * jnp.maximum(jnp.abs(_g), 1.0) + (_g == 0) * 1.0
        g_xattn = _g[0]
        g_ffn = _g[1]
        return (x, ctx_1024, g_xattn, g_ffn)
    x, ctx_1024, g_xattn, g_ffn = _rec_inputs()

    def _L0_xattn_setup():
        import jax, jax.numpy as jnp
        import numpy as np
        D_MODEL = 256
        N_HEAD = 16
        key = jax.random.key(seed)
        ks = jax.random.split(key, 12)
        B, T, D = (2, 512, D_MODEL)
        s = 1.0 / np.sqrt(D)
        return {'q': jax.random.normal(ks[0], (B, T, D), jnp.float32), 'k': jax.random.normal(ks[1], (B, T, D), jnp.float32), 'v': jax.random.normal(ks[2], (B, T, D), jnp.float32), 'w_q': jax.random.normal(ks[3], (D, D), jnp.float32) * s, 'b_q': jnp.zeros((D,), jnp.float32), 'w_k': jax.random.normal(ks[4], (D, D), jnp.float32) * s, 'b_k': jnp.zeros((D,), jnp.float32), 'w_v': jax.random.normal(ks[5], (D, D), jnp.float32) * s, 'b_v': jnp.zeros((D,), jnp.float32), 'w_o': jax.random.normal(ks[6], (D, D), jnp.float32) * s, 'b_o': jnp.zeros((D,), jnp.float32)}
    _L0_xattn_all = _L0_xattn_setup()
    _L0_xattn_in = {k: v for k, v in _L0_xattn_all.items() if k in ('w_q', 'b_q', 'w_k', 'b_k', 'w_v', 'b_v', 'w_o', 'b_o')}
    del _L0_xattn_all

    def _L0_ffn_setup():
        import jax, jax.numpy as jnp
        import numpy as np
        B, S, H, E = (2, 2048, 256, 8)
        SCALE = 0.5
        key = jax.random.key(seed)
        k1, k2 = jax.random.split(key)
        x = jax.random.normal(k1, (B, S, H), dtype=jnp.float32)
        gate_w = jax.random.normal(k2, (E, H), dtype=jnp.float32) * 0.02
        coeff = SCALE * (1.0 + 0.05 * jnp.arange(E, dtype=jnp.float32))
        expert_w = coeff[:, None, None] * jnp.eye(H, dtype=jnp.float32)
        return {'x': x, 'gate_w': gate_w, 'expert_w': expert_w}
    _L0_ffn_all = _L0_ffn_setup()
    _L0_ffn_in = {k: v for k, v in _L0_ffn_all.items() if k in ('gate_w', 'expert_w')}
    del _L0_ffn_all
    return {'x': x, 'ctx_1024': ctx_1024, 'g_xattn': g_xattn, 'g_ffn': g_ffn, 'L0_xattn_w_q': _L0_xattn_in['w_q'], 'L0_xattn_b_q': _L0_xattn_in['b_q'], 'L0_xattn_w_k': _L0_xattn_in['w_k'], 'L0_xattn_b_k': _L0_xattn_in['b_k'], 'L0_xattn_w_v': _L0_xattn_in['w_v'], 'L0_xattn_b_v': _L0_xattn_in['b_v'], 'L0_xattn_w_o': _L0_xattn_in['w_o'], 'L0_xattn_b_o': _L0_xattn_in['b_o'], 'L0_ffn_gate_w': _L0_ffn_in['gate_w'], 'L0_ffn_expert_w': _L0_ffn_in['expert_w']}

def reference(x, ctx_1024, g_xattn, g_ffn, L0_xattn_w_q, L0_xattn_b_q, L0_xattn_w_k, L0_xattn_b_k, L0_xattn_w_v, L0_xattn_b_v, L0_xattn_w_o, L0_xattn_b_o, L0_ffn_gate_w, L0_ffn_expert_w):
    import jax
    import jax.numpy as jnp

    def _L0_xattn_ref(q, k, v, w_q, b_q, w_k, b_k, w_v, b_v, w_o, b_o):
        import jax, jax.numpy as jnp
        import numpy as np
        D_MODEL = 256
        N_HEAD = 16
        B, T, D = q.shape
        H = N_HEAD
        nd = D // H
        qh = (q @ w_q + b_q).reshape(B, T, H, nd).transpose(0, 2, 1, 3)
        kh = (k @ w_k + b_k).reshape(B, T, H, nd).transpose(0, 2, 1, 3)
        vh = (v @ w_v + b_v).reshape(B, T, H, nd).transpose(0, 2, 1, 3)
        score = jnp.einsum('bhqd,bhkd->bhqk', qh, kh) / jnp.sqrt(jnp.float32(nd))
        causal = jnp.tril(jnp.ones((T, T), dtype=bool))
        score = jnp.where(causal, score, -jnp.inf)
        attn = jax.nn.softmax(score, axis=-2)
        out = jnp.einsum('bhqk,bhkd->bhqd', attn, vh)
        out = out.transpose(0, 2, 1, 3).reshape(B, T, D)
        return out @ w_o + b_o

    def _L0_ffn_ref(x, gate_w, expert_w):
        import jax, jax.numpy as jnp
        import numpy as np
        B, S, H, E = (2, 2048, 256, 8)
        SCALE = 0.5
        scores = jnp.einsum('bsh,eh->bse', x, gate_w)
        chosen = jnp.argmax(scores, axis=-1)
        onehot = jax.nn.one_hot(chosen, gate_w.shape[0], dtype=x.dtype)
        expert_out = jnp.einsum('bsh,efh->bsef', x, expert_w)
        return x + jnp.einsum('bsef,bse->bsf', expert_out, onehot)
    x = x + jnp.tanh(g_xattn[0]) * _L0_xattn_ref(_layernorm(x, axis=-1), ctx_1024, ctx_1024, L0_xattn_w_q, L0_xattn_b_q, L0_xattn_w_k, L0_xattn_b_k, L0_xattn_w_v, L0_xattn_b_v, L0_xattn_w_o, L0_xattn_b_o)
    x = x + jnp.tanh(g_ffn[0]) * _L0_ffn_ref(_layernorm(x, axis=-1), L0_ffn_gate_w, L0_ffn_expert_w)
    return x

_drawn_inputs = setup_inputs


def setup_inputs(seed=0):
    import zlib

    import numpy as np

    out = dict(_drawn_inputs(seed))
    spreads = {'L0_xattn_b_q': (0.0, 0.1),
     'L0_xattn_b_k': (0.0, 0.1),
     'L0_xattn_b_v': (0.0, 0.1),
     'L0_xattn_b_o': (0.0, 0.1)}
    factors = {}
    for name, (base, spread) in spreads.items():
        noise = np.random.default_rng([zlib.crc32(name.encode()), seed]).standard_normal(out[name].shape)
        drawn = base * np.exp(spread * noise) if base else spread * noise
        out[name] = jnp.asarray(drawn.astype(out[name].dtype))
    for name, factor in factors.items():
        out[name] = (out[name] * factor).astype(out[name].dtype)
    return out
```

```python
from contextlib import ExitStack

import concourse.bass as bass
from concourse import mybir

ALU = mybir.AluOpType
ACT = mybir.ActivationFunctionType
F32 = mybir.dt.float32
F32R = mybir.dt.float32r
BF16 = mybir.dt.bfloat16
AX_X = mybir.AxisListType.X

P = 128
EPS = 1e-5
NEG = -1e30


def attention_moe_kernel(nc, x, ctx, g_xattn, g_ffn, w_q, b_q, w_k, b_k, w_v, b_v, w_o, b_o,
                         gate_w, expert_w, out):
    B, T, D = x.shape
    E = gate_w.shape[0]
    HD = 16
    KD = D // P
    TT = T // P
    NT = B * TT
    PAIRS = P // (2 * HD)
    KB = 64
    NKB = T // KB
    TILES = KD * NKB * PAIRS
    BLOCKS = KD * NKB
    BANKS = 4
    RING = 4
    LAG = 3
    SCALE = HD ** -0.5
    WEIGHT_DMAS = 4 + 2 * KD + 2 + 1 + 2
    STACK_DMAS = 2 * 2 * 4
    assert SCALE == 0.25 and KD == 2 and NKB == 8 and TT == 4 and E == 8 and B >= 3
    PROJ = ("k", 0), ("k", 1), ("q", 0), ("q", 1)

    def queries(kb):
        return T - KB * kb

    def natural(v):
        return v.rearrange("p (kb i) -> p kb i", i=KB)

    def split_order(v, j):
        if PROJ[j][0] == "k":
            return v.rearrange("p (i kb) -> p kb i", kb=NKB)
        return natural(v)

    with ExitStack() as es:
        def sb(name, shape, dt=F32):
            return es.enter_context(nc.sbuf_tensor(name, shape, dt))

        def sem(name):
            return es.enter_context(nc.semaphore(name))

        x_all = sb("x_all", [P, NT, D])
        ctx_in = sb("ctx_in", [P, TT, D])
        xhat = sb("xhat", [P, TT, D])
        ctxT = sb("ctxT", [P, KD, T])
        xhatT = sb("xhatT", [P, KD, T])
        split = sb("split", [P, 4, 2, T], F32R)
        kstack = [sb(f"kstack{h}", [P, PAIRS, 2, T], F32R) for h in range(KD)]
        qstack = [sb(f"qstack{h}", [P, PAIRS, T], F32R) for h in range(KD)]
        v_rows = sb("v_rows", [P, 2, NKB, 2 * PAIRS, 2 * HD])
        v_scaled = sb("v_scaled", [P, RING, PAIRS, 2 * HD])
        probs = sb("probs", [P, RING, PAIRS, T])
        neg_max = sb("neg_max", [P, RING, PAIRS])
        z_sum = sb("z_sum", [P, RING, PAIRS])
        z_inv = sb("z_inv", [P, RING, PAIRS])
        attnT = sb("attnT", [P, KD, T])
        wq = sb("wq", [P, KD, D])
        wk = sb("wk", [P, KD, D])
        wv = sb("wv", [P, KD, D])
        wo = sb("wo", [P, KD, D])
        bq = sb("bq", [P, KD])
        bk = sb("bk", [P, KD])
        bv_all = sb("bv_all", [P, 2, D])
        bo_all = sb("bo_all", [P, D])
        gates_in = sb("gates_in", [P, 2])
        gates = sb("gates", [P, 2])
        identity = sb("identity", [P, P])
        identity_bf = sb("identity_bf", [P, P], BF16)
        causal_bf = sb("causal_bf", [P, KB], BF16)
        minus_half = sb("minus_half", [P, TT])
        stats = sb("stats", [P, TT, 6])
        mean_var = sb("mean_var", [P, TT, 2])
        var_eps = sb("var_eps", [P, TT])
        rstd = sb("rstd", [P, TT])
        gate_rows = sb("gate_rows", [E, D])
        gateT = sb("gateT", [P, KD, E])
        expert_rows = split[:].rearrange("p j h t -> p (j h t)").bitcast(F32).rearrange(
            "p (e d) -> p e d", d=D)
        expertT = sb("expertT", [P, KD, E, D])
        first_wins = sb("first_wins", [P, E])
        h_tile = sb("h_tile", [P, D])
        hT = sb("hT", [P, KD, P])
        acc = sb("acc", [P, D])
        best = sb("best", [P, 1])
        is_best = sb("is_best", [P, E])
        ranked = sb("ranked", [P, E])
        top_rank = sb("top_rank", [P, 1])
        onehot = sb("onehot", [P, E])

        scores_ps = es.enter_context(nc.psum_tensor("scores_ps", [P, BANKS, T], F32))
        attn_ps = es.enter_context(nc.psum_tensor("attn_ps", [P, KD, T], F32))
        misc_ps = es.enter_context(nc.psum_tensor("misc_ps", [P, 2, T], F32))

        split_dram = nc.dram_tensor("split_dram", [B, 4, 2, P, T], F32, kind="Internal").ap()

        weights_in = sem("weights_in")
        experts_in = sem("experts_in")
        tokens_in = sem("tokens_in")
        consts_zeroed = sem("consts_zeroed")
        consts_ready = sem("consts_ready")
        zeros_ready = sem("zeros_ready")
        gates_ready = sem("gates_ready")
        wq_scaled = sem("wq_scaled")
        wo_scaled = sem("wo_scaled")
        ln_stats = sem("ln_stats")
        ln_mean_var = sem("ln_mean_var")
        ln_var_eps = sem("ln_var_eps")
        ln_rstd = sem("ln_rstd")
        xhat_ready = sem("xhat_ready")
        resid_ready = sem("resid_ready")
        ctxT_filled = [sem(f"ctxT_filled{k}") for k in range(KD)]
        ctxT_copied = [sem(f"ctxT_copied{k}") for k in range(KD)]
        xhatT_filled = [sem(f"xhatT_filled{k}") for k in range(KD)]
        xhatT_copied = [sem(f"xhatT_copied{k}") for k in range(KD)]
        proj_filled = [sem(f"proj_filled_{a}{m}") for a, m in PROJ]
        proj_hi = [sem(f"proj_hi_{a}{m}") for a, m in PROJ]
        proj_lo = [sem(f"proj_lo_{a}{m}") for a, m in PROJ]
        split_stored = sem("split_stored")
        stack_loaded = [sem(f"stack_loaded{h}") for h in range(KD)]
        v_filled = [sem(f"v_filled{i}") for i in range(2)]
        v_copied = [sem(f"v_copied{i}") for i in range(2)]
        scores_done = sem("scores_done")
        half_scored = [sem(f"half_scored{h}") for h in range(KD)]
        max_done = sem("max_done")
        exp_done = sem("exp_done")
        zinv_done = sem("zinv_done")
        v_scaled_done = sem("v_scaled_done")
        pv_done = sem("pv_done")
        attn_copied = [sem(f"attn_copied{h}") for h in range(KD)]
        y_filled = [sem(f"y_filled{i}") for i in range(2)]
        y_added = [sem(f"y_added{i}") for i in range(2)]
        expertT_filled = sem("expertT_filled")
        expertT_copied = sem("expertT_copied")
        gateT_filled = sem("gateT_filled")
        gateT_copied = sem("gateT_copied")
        h_ready = sem("h_ready")
        hT_filled = sem("hT_filled")
        hT_copied = sem("hT_copied")
        logits_done = sem("logits_done")
        pick = sem("pick")
        experts_done = [sem(f"experts_done{c}") for c in range(4)]
        acc_step = sem("acc_step")
        row_ready = sem("row_ready")
        row_stored = sem("row_stored")

        x_t = x.rearrange("b (t p) d -> b p t d", p=P)
        ctx_t = ctx.rearrange("b (t p) d -> b p t d", p=P)
        out_t = out.rearrange("b (t p) d -> (b t) p d", p=P)

        block = es.enter_context(nc.Block())

        @block.sync
        def _(sp):
            def on_all(v):
                return v.rearrange("(a n) -> a n", a=1).partition_broadcast(P)

            def load_tokens(c):
                sp.dma_start(x_all[:, bass.ds(TT * c, TT), :],
                             x_t[bass.ds(c, 1)].rearrange("a p t d -> (a p) t d")).then_inc(tokens_in, 16)
                sp.dma_start(ctx_in[:], ctx_t[bass.ds(c, 1)].rearrange("a p t d -> (a p) t d"))\
                    .then_inc(tokens_in, 16)

            def store_split(c):
                for j in range(4):
                    sp.wait_ge(proj_lo[j], c + 1)
                    sp.wait_ge(proj_hi[j], c + 1)
                    sp.dma_start(split_dram[bass.ds(c, 1), j].rearrange("a h p t -> (a p) h t"),
                                 split[:, j].bitcast(F32)).then_inc(split_stored, 16)

            def load_stack(c, h):
                for a, stack in enumerate((kstack[h], qstack[h])):
                    for head in range(2):
                        for prod in range(4):
                            part = prod % 2 if a == 0 else prod // 2
                            src = split_dram[bass.ds(c, 1), 2 * a + h, part].rearrange(
                                "a (g s d) t -> s (a d) g t", s=2, d=HD)[head]
                            row = 64 * head + HD * prod
                            dst = stack[row:row + HD, :, head, :] if a == 0 else stack[row:row + HD, :, :]
                            sp.dma_start(dst.bitcast(F32), src).then_inc(stack_loaded[h], 16)

            load_tokens(0)
            for dst, w in ((wk, w_k), (wv, w_v), (wq, w_q), (wo, w_o)):
                sp.dma_start(dst[:], w.rearrange("(k p) n -> p k n", p=P)).then_inc(weights_in, 16)
            for dst, v in ((bq, b_q), (bk, b_k)):
                for k in range(KD):
                    sp.dma_start(dst[:, k:k + 1], v.rearrange("(k p a) -> k p a", p=P, a=1)[k])\
                        .then_inc(weights_in, 16)
            for i in range(2):
                sp.dma_start(bv_all[:, i, :], on_all(b_v)).then_inc(weights_in, 16)
            sp.dma_start(bo_all[:], on_all(b_o)).then_inc(weights_in, 16)
            for i, g in enumerate((g_xattn, g_ffn)):
                sp.dma_start(gates_in[:, i:i + 1], on_all(g)).then_inc(weights_in, 16)
            sp.dma_start(gate_rows[:], gate_w).then_inc(experts_in, 16)

            def iteration(b, first=False, last=False):
                if not last:
                    sp.wait_ge(ctxT_filled[0], b + 1)
                    sp.wait_ge(ctxT_filled[1], b + 1)
                    load_tokens(b + 1)
                if first:
                    store_split(b)
                    sp.wait_ge(split_stored, 64 * (b + 1))
                    load_stack(b, 0)
                else:
                    sp.wait_ge(half_scored[1], b)
                load_stack(b, 1)
                if not last:
                    store_split(b + 1)
                    sp.wait_ge(split_stored, 64 * (b + 2))
                    sp.wait_ge(half_scored[0], b + 1)
                    load_stack(b + 1, 0)

            iteration(0, first=True)
            with sp.Fori(1, B - 1) as b:
                iteration(b)
            sp.dma_start(expert_rows, expert_w.rearrange("e (k p) h -> p (e k) h", p=P))\
                .then_inc(experts_in, 16)
            iteration(B - 1, last=True)

            with sp.Fori(0, NT) as i:
                sp.wait_ge(row_ready, i + 1)
                sp.dma_start(out_t[bass.ds(i, 1)].rearrange("a p d -> (a p) d"),
                             x_all[:, bass.ds(i, 1), :].rearrange("p a d -> p (a d)"))\
                    .then_inc(row_stored, 16)
            sp.wait_ge(row_stored, 16 * NT)

        @block.gpsimd
        def _(pool):
            nc.gpsimd.memset(identity[:], 0.0)
            nc.gpsimd.memset(identity_bf[:], 0.0)
            nc.gpsimd.memset(causal_bf[:], 0.0)
            nc.gpsimd.memset(minus_half[:], -0.5).then_inc(consts_zeroed, 1)
            pool.wait_ge(consts_zeroed, 1)
            for m in (identity, identity_bf):
                nc.gpsimd.affine_select(out=m[:], in_=m[:], compare_op=ALU.not_equal, fill=1.0, base=0,
                                        pattern=[[-1, P]], channel_multiplier=1)
            for rows, base, done in ((P, KB, consts_zeroed), (KB, 0, consts_ready)):
                last = nc.gpsimd.affine_select(out=causal_bf[0:rows], in_=causal_bf[0:rows],
                                               compare_op=ALU.is_ge, fill=NEG, base=base,
                                               pattern=[[1, KB]], channel_multiplier=-1)
                last.then_inc(done, 1)
                pool.wait_ge(done, 2 if rows == P else 1)

            def rstd_of(c):
                pool.wait_ge(ln_var_eps, c + 1)
                nc.gpsimd.tensor_tensor(rstd[:], var_eps[:], minus_half[:], ALU.pow).then_inc(ln_rstd, 1)

            def residual(c):
                pool.wait_ge(xhat_ready, c + 1)
                for t in range(TT):
                    row = x_all[:, bass.ds(TT * c + t, 1), :].rearrange("p a d -> p (a d)")
                    last = nc.gpsimd.tensor_tensor(row, row, bo_all[:], ALU.add)
                last.then_inc(resid_ready, 1)

            def scale_v(b, blk):
                if blk < 0:
                    b, blk = b - 1, blk + BLOCKS
                pool.wait_ge(zinv_done, BLOCKS * b + blk + 1)
                if isinstance(b, int) and BLOCKS * b + blk < RING:
                    pass
                else:
                    pool.wait_ge(pv_done, BLOCKS * b + blk - RING + 1)
                if blk == 0:
                    pool.wait_ge(v_copied[0], b + 1)
                    pool.wait_ge(v_copied[1], b + 1)
                h, kb = divmod(blk, NKB)
                slot = blk % RING
                rows = v_rows[:, bass.ds(b % 2, 1), kb, PAIRS * h:PAIRS * (h + 1), :]
                rows = rows.rearrange("p a g d -> p (a g) d")
                nc.gpsimd.tensor_tensor(v_scaled[:, slot], rows,
                                        z_inv[:, slot, :].unsqueeze(2).to_broadcast([P, PAIRS, 2 * HD]),
                                        ALU.mult).then_inc(v_scaled_done, 1)

            def iteration(b, first=False, last=False):
                for blk in range(BLOCKS):
                    if not (first and blk < 2):
                        scale_v(b, blk - 2)
                    if blk == 2 and not last:
                        rstd_of(b + 1)
                    if blk == 4 and not last:
                        residual(b + 1)

            pool.wait_ge(wo_scaled, 1)
            rstd_of(0)
            residual(0)
            iteration(0, first=True)
            with pool.Fori(1, B - 1) as b:
                iteration(b)
            iteration(B - 1, last=True)
            scale_v(B, -2)
            scale_v(B, -1)

            with pool.Fori(0, NT) as i:
                rstd_of(i + B)

        @block.tensor
        def _(pe):
            def transpose_ctx(c, k):
                if k == 0:
                    pe.wait_ge(tokens_in, 32 * (c + 1))
                if not (isinstance(c, int) and c == 0):
                    pe.wait_ge(v_copied[k], c)
                for t in range(TT):
                    last = nc.tensor.transpose(misc_ps[:, k, P * t:P * (t + 1)],
                                               ctx_in[:, t, P * k:P * (k + 1)], identity[:])
                last.then_inc(ctxT_filled[k], 1)

            def transpose_xhat(c, k, after_y):
                if k == 0:
                    pe.wait_ge(xhat_ready, c + 1)
                if after_y:
                    pe.wait_ge(y_added[k], c - 1)
                else:
                    pe.wait_ge(proj_lo[k], c + 1)
                for t in range(TT):
                    last = nc.tensor.transpose(misc_ps[:, k, P * t:P * (t + 1)],
                                               xhat[:, t, P * k:P * (k + 1)], identity[:])
                last.then_inc(xhatT_filled[k], 1)

            def project(c, j):
                a, m = PROJ[j]
                src, w = (ctxT, wk) if a == "k" else (xhatT, wq)
                for k in range(KD):
                    pe.wait_ge(ctxT_copied[k] if a == "k" else xhatT_copied[k], c + 1)
                for k in range(KD):
                    last = nc.tensor.matmul(misc_ps[:, m, :], w[:, k, P * m:P * (m + 1)], src[:, k, :],
                                            start=(k == 0), stop=(k == KD - 1))
                last.then_inc(proj_filled[j], 1)

            def project_v(c, i):
                pe.wait_ge(proj_lo[2 + i], c + 1)
                for t in range(2):
                    cols = slice(P * (2 * i + t), P * (2 * i + t + 1))
                    for k in range(KD):
                        last = nc.tensor.matmul(misc_ps[:, i, D * t:D * (t + 1)], ctxT[:, k, cols],
                                                wv[:, k, :], start=(k == 0), stop=(k == KD - 1))
                last.then_inc(v_filled[i], 1)

            def project_out(c, i, bank_free, count):
                pe.wait_ge(bank_free, count)
                for h in range(KD):
                    pe.wait_ge(attn_copied[h], c + 1)
                for t in range(2):
                    cols = slice(P * (2 * i + t), P * (2 * i + t + 1))
                    for h in range(KD):
                        last = nc.tensor.matmul(misc_ps[:, i, D * t:D * (t + 1)], attnT[:, h, cols],
                                                wo[:, h, :], start=(h == 0), stop=(h == KD - 1))
                last.then_inc(y_filled[i], 1)

            def keys_of(h, g, kb):
                return kstack[h][:, g].rearrange("p s (i kb) -> p (s i) kb", kb=NKB)[:, :, kb]

            def score(b, n, first):
                blk, g = divmod(n, PAIRS)
                h, kb = divmod(blk, NKB)
                L = queries(kb)
                if kb == 0 and g == 0:
                    pe.wait_ge(stack_loaded[h], 16 * STACK_DMAS * (b + 1))
                if not (first and n < BANKS):
                    pe.wait_ge(exp_done, TILES * b + n - BANKS + 1)
                s = scores_ps[:, n % BANKS, :]
                product = nc.tensor.matmul(s[:, 0:L], keys_of(h, g, kb),
                                           qstack[h][:, g, KB * kb:T], start=True, stop=False)
                if n % (NKB * PAIRS) == NKB * PAIRS - 1:
                    product.then_inc(half_scored[h], 1)
                nc.tensor.matmul(s[:, 0:KB], identity_bf[:], causal_bf[:], start=False, stop=True)\
                    .then_inc(scores_done, 1)

            def times_v(b, blk, first=False):
                if blk < 0:
                    b, blk = b - 1, blk + BLOCKS
                h, kb = divmod(blk, NKB)
                if kb == 0 and not first:
                    pe.wait_ge(attn_copied[h], b)
                pe.wait_ge(v_scaled_done, BLOCKS * b + blk + 1)
                slot = blk % RING
                for g in range(PAIRS):
                    last = nc.tensor.matmul(attn_ps[32 * g:32 * (g + 1), h, KB * kb:T],
                                            v_scaled[:, slot, g, :], probs[:, slot, g, 0:queries(kb)],
                                            start=(kb == 0), stop=(kb == NKB - 1))
                last.then_inc(pv_done, 1)

            def prepare(c, n, after_y=True):
                if n == 1:
                    transpose_ctx(c, 0)
                if n == 2:
                    transpose_ctx(c, 1)
                if n == 6:
                    project(c, 0)
                if n == 11:
                    project(c, 1)
                if n == 18:
                    transpose_xhat(c, 0, after_y)
                if n == 20:
                    transpose_xhat(c, 1, after_y)
                if n == 24:
                    project(c, 2)
                if n == 28:
                    project(c, 3)
                if n == 34:
                    project_v(c, 0)
                if n == 38:
                    project_v(c, 1)

            def iteration(b, first=False, last=False):
                for n in range(TILES):
                    score(b, n, first)
                    if n % PAIRS == 0 and not (first and n < LAG * PAIRS):
                        times_v(b, n // PAIRS - LAG, first)
                    if not first and n in (14, 16):
                        i = (n - 14) // 2
                        if last:
                            project_out(b - 1, i, v_copied[i], B)
                        else:
                            project_out(b - 1, i, proj_lo[i], b + 2)
                    if not last:
                        prepare(b + 1, n, after_y=not first)

            pe.wait_ge(consts_ready, 1)
            for n in range(TILES):
                if n == 6:
                    pe.wait_ge(weights_in, 16 * WEIGHT_DMAS)
                    pe.wait_ge(wq_scaled, 2)
                prepare(0, n, after_y=False)
            pe.wait_ge(zeros_ready, 1)
            iteration(0, first=True)
            with pe.Fori(1, B - 1) as b:
                iteration(b)
            iteration(B - 1, last=True)
            for blk in range(-LAG, 0):
                times_v(B, blk)
            for i in range(2):
                project_out(B - 1, i, y_added[i], B - 1)

            pe.wait_ge(experts_in, 32)
            for e in range(E):
                if e < BANKS:
                    pe.wait_ge(exp_done, B * TILES)
                else:
                    pe.wait_ge(expertT_copied, e - BANKS + 1)
                for k in range(KD):
                    for f in range(KD):
                        last = nc.tensor.transpose(
                            scores_ps[:, e % BANKS, D * k + P * f:D * k + P * (f + 1)],
                            expert_rows[:, KD * e + f, P * k:P * (k + 1)], identity[:])
                last.then_inc(expertT_filled, 1)
            pe.wait_ge(attn_copied[0], B)
            for k in range(KD):
                last = nc.tensor.transpose(attn_ps[:, 0, E * k:E * (k + 1)],
                                           gate_rows[:, P * k:P * (k + 1)], identity[0:E, 0:E])
            last.then_inc(gateT_filled, 1)
            pe.wait_ge(gateT_copied, 1)
            pe.wait_ge(expertT_copied, E)
            pe.wait_ge(y_added[0], B)
            pe.wait_ge(y_added[1], B)
            with pe.Fori(0, NT) as i:
                pe.wait_ge(h_ready, i + 1)
                for k in range(KD):
                    last = nc.tensor.transpose(misc_ps[:, 0, P * k:P * (k + 1)],
                                               h_tile[:, P * k:P * (k + 1)], identity[:])
                last.then_inc(hT_filled, 1)
                pe.wait_ge(hT_copied, i + 1)
                for k in range(KD):
                    last = nc.tensor.matmul(misc_ps[:, 1, 0:E], hT[:, k, :], gateT[:, k, :],
                                            start=(k == 0), stop=(k == KD - 1))
                last.then_inc(logits_done, 1)
                for c in range(4):
                    for k in range(KD):
                        last = nc.tensor.matmul(
                            scores_ps[:, c, :], hT[:, k, :],
                            expertT[:, k, 2 * c:2 * c + 2, :].rearrange("p e f -> p (e f)"),
                            start=(k == 0), stop=(k == KD - 1))
                    last.then_inc(experts_done[c], 1)

        @block.scalar
        def _(act):
            act.wait_ge(weights_in, 16 * WEIGHT_DMAS)
            nc.scalar.activation(gates[:], gates_in[:], ACT.Tanh).then_inc(gates_ready, 1)
            nc.scalar.mul(wq[:], wq[:], SCALE).then_inc(wq_scaled, 1)
            nc.scalar.mul(bq[:], bq[:], SCALE).then_inc(wq_scaled, 1)
            act.wait_ge(wq_scaled, 2)

            def copy(dst, src, filled, count, copied):
                act.wait_ge(filled, count)
                nc.scalar.copy(dst, src).then_inc(copied, 1)

            def split_hi(c, j):
                a, m = PROJ[j]
                act.wait_ge(proj_filled[j], c + 1)
                if not (isinstance(c, int) and c == 0):
                    act.wait_ge(split_stored, 64 * c)
                nc.scalar.activation(split_order(split[:, j, 0, :], j), natural(misc_ps[:, m, :]),
                                     ACT.Identity,
                                     bias=(bk if a == "k" else bq)[:, m:m + 1]).then_inc(proj_hi[j], 1)

            def copy_attn(b, h):
                act.wait_ge(pv_done, BLOCKS * b + NKB * (h + 1))
                if not (isinstance(b, int) and b == 0):
                    act.wait_ge(y_filled[1], b)
                nc.scalar.copy(attnT[:, h, :], attn_ps[:, h, :]).then_inc(attn_copied[h], 1)

            def exps(b, n, first):
                blk, g = divmod(n, PAIRS)
                slot = blk % RING
                act.wait_ge(max_done, TILES * b + n + 1)
                if g == 0 and not (first and blk < RING):
                    act.wait_ge(pv_done, BLOCKS * b + blk - RING + 1)
                L = queries(blk % NKB)
                nc.scalar.activation(probs[:, slot, g, 0:L], scores_ps[:, n % BANKS, 0:L], ACT.Exp,
                                     bias=neg_max[:, slot, g:g + 1],
                                     accum_out=z_sum[:, slot, g:g + 1]).then_inc(exp_done, 1)

            def prepare(c, n):
                if n == 3:
                    if not (isinstance(c, int) and c == 0):
                        act.wait_ge(v_filled[1], c)
                    copy(ctxT[:, 0, :], misc_ps[:, 0, :], ctxT_filled[0], c + 1, ctxT_copied[0])
                if n == 8:
                    split_hi(c, 0)
                if n == 13:
                    split_hi(c, 1)
                if n == 20:
                    if not (isinstance(c, int) and c == 0):
                        act.wait_ge(proj_filled[3], c)
                    copy(xhatT[:, 0, :], misc_ps[:, 0, :], xhatT_filled[0], c + 1, xhatT_copied[0])
                if n == 26:
                    split_hi(c, 2)
                if n == 31:
                    split_hi(c, 3)

            def iteration(b, first=False, last=False):
                for n in range(TILES):
                    if not last:
                        prepare(b + 1, n)
                    if n == 11 and not first:
                        copy_attn(b - 1, 1)
                    if n == 43:
                        copy_attn(b, 0)
                    exps(b, n, first)

            for n in range(TILES):
                prepare(0, n)
            iteration(0, first=True)
            with act.Fori(1, B - 1) as b:
                iteration(b)
            iteration(B - 1, last=True)
            copy_attn(B - 1, 1)

            for e in range(E):
                act.wait_ge(expertT_filled, e + 1)
                nc.scalar.copy(expertT[:, :, e, :],
                               scores_ps[:, e % BANKS, :].rearrange("p (k f) -> p k f", k=KD))\
                    .then_inc(expertT_copied, 1)
            copy(gateT[:].rearrange("p k e -> p (k e)"), attn_ps[:, 0, 0:KD * E], gateT_filled, 1,
                 gateT_copied)
            with act.Fori(0, NT) as i:
                copy(hT[:].rearrange("p k t -> p (k t)"), misc_ps[:, 0, 0:D], hT_filled, i + 1, hT_copied)

        @block.vector
        def _(dve):
            for h in range(KD):
                nc.vector.memset(kstack[h][0:64, :, 1, :].bitcast(F32), 0.0)
                nc.vector.memset(kstack[h][64:128, :, 0, :].bitcast(F32), 0.0)
            nc.vector.memset(v_rows[:], 0.0).then_inc(zeros_ready, 1)
            for e in range(E):
                nc.vector.memset(first_wins[:, e:e + 1], float(E - e))
            dve.wait_ge(gates_ready, 1)
            nc.vector.tensor_scalar(wo[:], wo[:], gates[:, 0:1], None, ALU.mult)
            nc.vector.tensor_scalar(bo_all[:], bo_all[:], gates[:, 0:1], None, ALU.mult)\
                .then_inc(wo_scaled, 1)

            def tile_stats(c, t, row):
                nc.vector.bn_stats(stats[:, t, :], row)

            def split_lo(c, j):
                a, m = PROJ[j]
                dve.wait_ge(proj_hi[j], c + 1)
                nc.vector.scalar_tensor_tensor(
                    split_order(split[:, j, 1, :], j), natural(misc_ps[:, m, :]),
                    (bk if a == "k" else bq)[:, m:m + 1],
                    split_order(split[:, j, 0, :], j).bitcast(F32), ALU.add, ALU.subtract).then_inc(proj_lo[j], 1)

            def copy_v(c, i):
                dve.wait_ge(v_filled[i], c + 1)
                for s in range(2):
                    for head in range(2):
                        dst = v_rows[64 * head:64 * (head + 1), bass.ds(c % 2, 1),
                                     4 * i + s:4 * i + s + 3:2, :, HD * head:HD * (head + 1)]
                        src = misc_ps[64 * s:64 * (s + 1), i, :].rearrange(
                            "p (t g s d) -> p s t g d", t=2, s=2, d=HD)[:, head]
                        bias = bv_all[64 * s:64 * (s + 1)].rearrange(
                            "p t (g s d) -> p s t g d", s=2, d=HD)[:, head]
                        last = nc.vector.tensor_tensor(dst.rearrange("p a t g d -> p (a t) g d"), src,
                                                       bias, ALU.add)
                last.then_inc(v_copied[i], 1)

            def add_y(b, i):
                dve.wait_ge(y_filled[i], b + 1)
                dve.wait_ge(resid_ready, b + 1)
                rows = x_all[:, bass.ds(TT * b + 2 * i, 2), :]
                nc.vector.tensor_tensor(rows, misc_ps[:, i, :].rearrange("p (t d) -> p t d", t=2), rows,
                                        ALU.add).then_inc(y_added[i], 1)

            def maxes(b, n, first):
                blk, g = divmod(n, PAIRS)
                dve.wait_ge(scores_done, TILES * b + n + 1)
                nc.vector.tensor_reduce(neg_max[:, blk % RING, g:g + 1],
                                        scores_ps[:, n % BANKS, 0:queries(blk % NKB)], AX_X, ALU.max,
                                        negate=True).then_inc(max_done, 1)

            def invert_z(b, blk):
                if blk < 0:
                    b, blk = b - 1, blk + BLOCKS
                dve.wait_ge(exp_done, TILES * b + PAIRS * (blk + 1))
                nc.vector.reciprocal(z_inv[:, blk % RING, :], z_sum[:, blk % RING, :])\
                    .then_inc(zinv_done, 1)

            def prepare(c, n):
                if n < TT:
                    if n == 0:
                        dve.wait_ge(tokens_in, 32 * (c + 1))
                    row = x_all[:, bass.ds(TT * c + n, 1), :].rearrange("p a d -> p (a d)")
                    last = nc.vector.bn_stats(stats[:, n, :], row)
                    if n == TT - 1:
                        last.then_inc(ln_stats, 1)
                if n == 5:
                    dve.wait_ge(ln_stats, c + 1)
                    if not (isinstance(c, int) and c == 0):
                        dve.wait_ge(v_filled[1], c)
                    dve.wait_ge(ctxT_filled[1], c + 1)
                    nc.vector.tensor_copy(ctxT[:, 1, :], misc_ps[:, 1, :]).then_inc(ctxT_copied[1], 1)
                    for t in range(TT):
                        last = nc.vector.bn_aggr(mean_var[:, t, :], stats[:, t, :])
                    last.then_inc(ln_mean_var, 1)
                if n == 7:
                    dve.wait_ge(ln_mean_var, c + 1)
                    nc.vector.tensor_scalar(var_eps[:], mean_var[:, :, 1], EPS, None, ALU.add)\
                        .then_inc(ln_var_eps, 1)
                if n == 10:
                    split_lo(c, 0)
                if n == 15:
                    split_lo(c, 1)
                if 11 <= n < 11 + TT:
                    t = n - 11
                    if t == 0:
                        dve.wait_ge(ln_rstd, c + 1)
                        if not (isinstance(c, int) and c == 0):
                            dve.wait_ge(xhatT_filled[1], c)
                    row = x_all[:, bass.ds(TT * c + t, 1), :].rearrange("p a d -> p (a d)")
                    last = nc.vector.tensor_scalar(xhat[:, t, :], row, mean_var[:, t, 0:1],
                                                   rstd[:, t:t + 1], ALU.subtract, ALU.mult)
                    if t == TT - 1:
                        last.then_inc(xhat_ready, 1)
                if n == 22:
                    dve.wait_ge(xhatT_filled[1], c + 1)
                    if not (isinstance(c, int) and c == 0):
                        dve.wait_ge(proj_filled[3], c)
                    nc.vector.tensor_copy(xhatT[:, 1, :], misc_ps[:, 1, :]).then_inc(xhatT_copied[1], 1)
                if n == 28:
                    split_lo(c, 2)
                if n == 33:
                    split_lo(c, 3)
                if n == 38:
                    copy_v(c, 0)
                if n == 44:
                    copy_v(c, 1)

            def iteration(b, first=False, last=False):
                for n in range(TILES):
                    if not last:
                        prepare(b + 1, n)
                    if n in (18, 20) and not first:
                        add_y(b - 1, (n - 18) // 2)
                    if n % PAIRS == 0 and not (first and n < 2 * PAIRS):
                        invert_z(b, n // PAIRS - 2)
                    maxes(b, n, first)

            for n in range(TILES):
                if n == 38:
                    dve.wait_ge(zeros_ready, 1)
                prepare(0, n)
            iteration(0, first=True)
            with dve.Fori(1, B - 1) as b:
                iteration(b)
            iteration(B - 1, last=True)
            invert_z(B, -2)
            invert_z(B, -1)
            for i in range(2):
                add_y(B - 1, i)
            for i in range(2):
                dve.wait_ge(y_added[i], B)

            PICKS = 4
            with dve.Fori(0, NT) as i:
                row = x_all[:, bass.ds(i, 1), :].rearrange("p a d -> p (a d)")
                nc.vector.bn_stats(stats[:, 0, :], row).then_inc(ln_stats, 1)
                dve.wait_ge(ln_stats, B + i + 1)
                nc.vector.memset(best[:], 0.0)
                nc.vector.bn_aggr(mean_var[:, 0, :], stats[:, 0, :]).then_inc(ln_mean_var, 1)
                dve.wait_ge(ln_mean_var, B + i + 1)
                nc.vector.tensor_scalar(var_eps[:, 0:1], mean_var[:, 0, 1:2], EPS, None, ALU.add)\
                    .then_inc(ln_var_eps, 1)
                dve.wait_ge(ln_rstd, B + i + 1)
                nc.vector.tensor_scalar(h_tile[:], row, mean_var[:, 0, 0:1], rstd[:, 0:1], ALU.subtract,
                                        ALU.mult).then_inc(h_ready, 1)
                dve.wait_ge(logits_done, i + 1)
                logits = misc_ps[:, 1, 0:E]
                nc.vector.reduce_max(best[:], logits, AX_X).then_inc(pick, 1)
                dve.wait_ge(pick, PICKS * i + 1)
                nc.vector.scalar_tensor_tensor(ranked[:], logits, best[:], first_wins[:], ALU.is_equal,
                                               ALU.mult).then_inc(pick, 1)
                dve.wait_ge(pick, PICKS * i + 2)
                nc.vector.reduce_max(top_rank[:], ranked[:], AX_X).then_inc(pick, 1)
                dve.wait_ge(pick, PICKS * i + 3)
                nc.vector.tensor_scalar(onehot[:], ranked[:], top_rank[:], None, ALU.is_equal)\
                    .then_inc(pick, 1)
                dve.wait_ge(pick, PICKS * i + 4)
                for e in range(E):
                    if e % 2 == 0:
                        dve.wait_ge(experts_done[e // 2], i + 1)
                    if e:
                        dve.wait_ge(acc_step, E * i + e)
                    nc.vector.scalar_tensor_tensor(
                        acc[:], scores_ps[:, e // 2, D * (e % 2):D * (e % 2 + 1)], onehot[:, e:e + 1],
                        h_tile[:] if e == 0 else acc[:], ALU.mult, ALU.add).then_inc(acc_step, 1)
                dve.wait_ge(acc_step, E * i + E)
                nc.vector.scalar_tensor_tensor(row, acc[:], gates[:, 1:2], row, ALU.mult, ALU.add)\
                    .then_inc(row_ready, 1)


_INS = ["x", "ctx_1024", "g_xattn", "g_ffn", "L0_xattn_w_q", "L0_xattn_b_q", "L0_xattn_w_k",
        "L0_xattn_b_k", "L0_xattn_w_v", "L0_xattn_b_v", "L0_xattn_w_o", "L0_xattn_b_o",
        "L0_ffn_gate_w", "L0_ffn_expert_w"]


def kernel(**inputs):
    import numpy as _np
    import concourse.bacc as _bacc
    from concourse import mybir as _mybir
    from concourse.bass_utils import run_bass_kernel_spmd as _run

    nc = _bacc.Bacc("TRN2", target_bir_lowering=False, num_devices=1)
    arrays, args = {}, []
    for name in _INS:
        a = _np.ascontiguousarray(inputs[name])
        arrays[f"in_{name}"] = a
        args.append(nc.dram_tensor(f"in_{name}", a.shape, _mybir.dt.from_np(a.dtype),
                                   kind="ExternalInput").ap())
    shape = tuple(inputs["x"].shape)
    args.append(nc.dram_tensor("out_x", shape, _mybir.dt.float32, kind="ExternalOutput").ap())
    attention_moe_kernel(nc, *args)
    r = _run(nc, [arrays], core_ids=[0])
    return r.results[0]["out_x"]
```

```python
from contextlib import ExitStack

import concourse.bass as bass
from concourse import mybir

ALU = mybir.AluOpType
ACT = mybir.ActivationFunctionType
F32 = mybir.dt.float32
F32R = mybir.dt.float32r
BF16 = mybir.dt.bfloat16
I32 = mybir.dt.int32
U32 = mybir.dt.uint32
AX_X = mybir.AxisListType.X

P = 128
EPS = 1e-5
NEG = -1e30


def attention_moe_kernel(nc, x, ctx, g_xattn, g_ffn, w_q, b_q, w_k, b_k, w_v, b_v, w_o, b_o,
                         gate_w, expert_w, out):
    B, T, D = x.shape
    E = gate_w.shape[0]
    HD = 16
    KD = D // P
    TT = T // P
    NT = B * TT
    PAIRS = P // (2 * HD)
    KB = 64
    NKB = T // KB
    TILES = KD * NKB * PAIRS
    BLOCKS = KD * NKB
    BANKS = 4
    RING = 4
    LAG = 3
    SCALE = HD ** -0.5
    WEIGHT_DMAS = 4 + 2 * KD + 2 + 1 + 2
    STACK_DMAS = 2 * 2 * 4
    assert SCALE == 0.25 and KD == 2 and NKB == 8 and TT == 4 and E == 8 and B >= 3
    ROW = D + 4
    ID, MEAN, VAR, RSTD = D, D + 1, D + 2, D + 3
    REGION = B * T + P
    SLOTS = 8
    STEPS = -(-(NT + E) // SLOTS)
    ROUTE_STEPS = 6
    ROUTED = STEPS * SLOTS
    PROJ = ("k", 0), ("k", 1), ("q", 0), ("q", 1)

    def queries(kb):
        return T - KB * kb

    def natural(v):
        return v.rearrange("p (kb i) -> p kb i", i=KB)

    def split_order(v, j):
        if PROJ[j][0] == "k":
            return v.rearrange("p (i kb) -> p kb i", kb=NKB)
        return natural(v)

    with ExitStack() as es:
        def sb(name, shape, dt=F32):
            return es.enter_context(nc.sbuf_tensor(name, shape, dt))

        def sem(name):
            return es.enter_context(nc.semaphore(name))

        x_ring = sb("x_ring", [P, 4 * TT, D])
        ctx_in = sb("ctx_in", [P, TT, D])
        xhat = sb("xhat", [P, TT, D])
        ctxT = sb("ctxT", [P, KD, T])
        xhatT = sb("xhatT", [P, KD, T])
        split = sb("split", [P, 4, 2, T], F32R)
        kstack = [sb(f"kstack{h}", [P, PAIRS, 2, T], F32R) for h in range(KD)]
        qstack = [sb(f"qstack{h}", [P, PAIRS, T], F32R) for h in range(KD)]
        v_rows = sb("v_rows", [P, 2, NKB, 2 * PAIRS, 2 * HD])
        v_scaled = sb("v_scaled", [P, RING, PAIRS, 2 * HD])
        probs = sb("probs", [P, RING, PAIRS, T])
        neg_max = sb("neg_max", [P, RING, PAIRS])
        z_sum = sb("z_sum", [P, RING, PAIRS])
        z_inv = sb("z_inv", [P, RING, PAIRS])
        attnT = sb("attnT", [P, KD, T])
        wq = sb("wq", [P, KD, D])
        wk = sb("wk", [P, KD, D])
        wv = sb("wv", [P, KD, D])
        wo = sb("wo", [P, KD, D])
        bq = sb("bq", [P, KD])
        bk = sb("bk", [P, KD])
        bv_all = sb("bv_all", [P, 2, D])
        bo_all = sb("bo_all", [P, D])
        gates_in = sb("gates_in", [P, 2])
        gates = sb("gates", [P, 2])
        identity = sb("identity", [P, P])
        identity_bf = sb("identity_bf", [P, P], BF16)
        causal_bf = sb("causal_bf", [P, KB], BF16)
        minus_half = sb("minus_half", [P, TT])
        stats = sb("stats", [P, TT, 6])
        mean_var = sb("mean_var", [P, TT, 2])
        var_eps = sb("var_eps", [P, TT])
        rstd = sb("rstd", [P, TT])
        ln_fence = sb("ln_fence", [P, 1])
        x1_bn = sb("x1_bn", [P, TT, 6])
        x1_eps = sb("x1_eps", [P, TT])
        gate_rows = sb("gate_rows", [E, D])
        gateT = sb("gateT", [P, KD, E])
        expert_rows = split[:].rearrange("p j h t -> p (j h t)").bitcast(F32).rearrange(
            "p (e d) -> p e d", d=D)
        expertT = sb("expertT", [P, KD, E, D])
        first_wins = sb("first_wins", [P, TT, E])
        x1_rows = sb("x1_rows", [P, TT, ROW])
        x1T = sb("x1T", [P, KD, T])
        gate_mean = sb("gate_mean", [E, 1])
        best = sb("best", [P, TT])
        ranked = sb("ranked", [P, TT, E])
        top_rank = sb("top_rank", [P, TT])
        onehot = sb("onehot", [P, TT, E], BF16)
        batch_seen = sb("batch_seen", [P, E], BF16)
        seen = sb("seen", [P, E], BF16)
        place = sb("place", [P, TT, E])
        dest_f = sb("dest_f", [P, TT])
        dest = sb("dest", [P, TT], U32)
        ids = sb("ids", [P, NT], U32)
        region_base = sb("region_base", [P, TT, E])
        earlier_bf = sb("earlier_bf", [P, P], BF16)
        ones_bf = sb("ones_bf", [P, P], BF16)
        padding = sb("padding", [P, ROW])
        thresholds = sb("thresholds", [1, E, NT])
        upto = sb("upto", [1, E, E])
        tile_no = sb("tile_no", [1, ROUTED, E])
        past = sb("past", [1, E, NT])
        tiles_of = sb("tiles_of", [1, E])
        tiles_upto = sb("tiles_upto", [1, E, E])
        ends = sb("ends", [1, E])
        ended = sb("ended", [1, ROUTED, E])
        ended_tiles = sb("ended_tiles", [1, ROUTED, E])
        expert_f = sb("expert_f", [1, ROUTED])
        first_tile = sb("first_tile", [1, ROUTED])
        in_region = sb("in_region", [1, ROUTED])
        row_f = sb("row_f", [1, ROUTED])
        tile_expert = sb("tile_expert", [1, ROUTED], I32)
        tile_row = sb("tile_row", [1, ROUTED], I32)
        pad_row = sb("pad_row", [1, E], I32)
        rows_in = sb("rows_in", [P, SLOTS, ROW])
        v_flat = v_rows[:].rearrange("p a k g d -> p (a k g d)")
        h_rows = v_flat[:, 0:SLOTS * D].rearrange("p (s d) -> p s d", d=D)
        hT = v_flat[:, SLOTS * D:(SLOTS + 4) * D].rearrange("p (s k t) -> p s k t", s=4, k=KD)

        scores_ps = es.enter_context(nc.psum_tensor("scores_ps", [P, BANKS, T], F32))
        attn_ps = es.enter_context(nc.psum_tensor("attn_ps", [P, KD, T], F32))
        misc_ps = es.enter_context(nc.psum_tensor("misc_ps", [P, 2, T], F32))

        split_dram = nc.dram_tensor("split_dram", [B, 4, 2, P, T], F32, kind="Internal").ap()
        regions = nc.dram_tensor("regions", [E * REGION + P, ROW], F32, kind="Internal").ap()

        weights_in = sem("weights_in")
        experts_in = sem("experts_in")
        tokens_in = sem("tokens_in")
        consts_zeroed = sem("consts_zeroed")
        consts_ready = sem("consts_ready")
        zeros_ready = sem("zeros_ready")
        gates_ready = sem("gates_ready")
        wq_scaled = sem("wq_scaled")
        wo_scaled = sem("wo_scaled")
        ln_stats = sem("ln_stats")
        ln_mean_var = sem("ln_mean_var")
        ln_var_eps = sem("ln_var_eps")
        ln_rstd = sem("ln_rstd")
        xhat_ready = sem("xhat_ready")
        resid_ready = sem("resid_ready")
        ctxT_filled = [sem(f"ctxT_filled{k}") for k in range(KD)]
        ctxT_copied = [sem(f"ctxT_copied{k}") for k in range(KD)]
        xhatT_filled = [sem(f"xhatT_filled{k}") for k in range(KD)]
        xhatT_copied = [sem(f"xhatT_copied{k}") for k in range(KD)]
        proj_filled = [sem(f"proj_filled_{a}{m}") for a, m in PROJ]
        proj_hi = [sem(f"proj_hi_{a}{m}") for a, m in PROJ]
        proj_lo = [sem(f"proj_lo_{a}{m}") for a, m in PROJ]
        split_stored = sem("split_stored")
        stack_loaded = [sem(f"stack_loaded{h}") for h in range(KD)]
        v_filled = [sem(f"v_filled{i}") for i in range(2)]
        v_copied = [sem(f"v_copied{i}") for i in range(2)]
        scores_done = sem("scores_done")
        half_scored = [sem(f"half_scored{h}") for h in range(KD)]
        max_done = sem("max_done")
        exp_done = sem("exp_done")
        zinv_done = sem("zinv_done")
        v_scaled_done = sem("v_scaled_done")
        pv_done = sem("pv_done")
        attn_copied = [sem(f"attn_copied{h}") for h in range(KD)]
        y_filled = [sem(f"y_filled{i}") for i in range(2)]
        y_added = [sem(f"y_added{i}") for i in range(2)]
        expertT_filled = sem("expertT_filled")
        expertT_copied = sem("expertT_copied")
        gateT_filled = sem("gateT_filled")
        gateT_copied = sem("gateT_copied")
        gate_step = sem("gate_step")
        gate_centred = sem("gate_centred")
        x1T_filled = [sem(f"x1T_filled{k}") for k in range(KD)]
        x1T_copied = [sem(f"x1T_copied{k}") for k in range(KD)]
        x1_stats = sem("x1_stats")
        x1_mean_var = sem("x1_mean_var")
        x1_var_eps = sem("x1_var_eps")
        x1_rstd = sem("x1_rstd")
        logits_filled = sem("logits_filled")
        logits_read = sem("logits_read")
        route = sem("route")
        onehot_ready = sem("onehot_ready")
        rank_filled = sem("rank_filled")
        rank_read = sem("rank_read")
        seen_ready = sem("seen_ready")
        dest_ready = sem("dest_ready")
        regions_stored = sem("regions_stored")
        padding_ready = sem("padding_ready")
        padding_stored = sem("padding_stored")
        counts_filled = sem("counts_filled")
        plan = sem("plan")
        plan_ready = sem("plan_ready")
        tile_loaded = [sem(f"tile_loaded{s}") for s in range(SLOTS)]
        h_ready = [sem(f"h_ready{s}") for s in range(SLOTS)]
        hT_filled = [sem(f"hT_filled{s}") for s in range(SLOTS)]
        hT_copied = [sem(f"hT_copied{s}") for s in range(SLOTS)]
        expert_filled = [sem(f"expert_filled{s}") for s in range(SLOTS)]
        expert_read = [sem(f"expert_read{s}") for s in range(SLOTS)]
        row_ready = [sem(f"row_ready{s}") for s in range(SLOTS)]
        row_stored = [sem(f"row_stored{s}") for s in range(SLOTS)]

        x_t = x.rearrange("b (t p) d -> b p t d", p=P)
        ctx_t = ctx.rearrange("b (t p) d -> b p t d", p=P)
        out_rows = out.rearrange("b t d -> (b t) d")
        hT_banks = [scores_ps[:, i, 0:D] for i in range(4)]
        expert_banks = [attn_ps[:, 0, 0:D], attn_ps[:, 1, 0:D], misc_ps[:, 0, 0:D], misc_ps[:, 1, 0:D]]

        block = es.enter_context(nc.Block())

        @block.sync
        def _(sp):
            def on_all(v):
                return v.rearrange("(a n) -> a n", a=1).partition_broadcast(P)

            def load_tokens(c):
                sp.dma_start(x_ring[:, bass.ds(TT * (c % 4), TT), :],
                             x_t[bass.ds(c, 1)].rearrange("a p t d -> (a p) t d")).then_inc(tokens_in, 16)
                sp.dma_start(ctx_in[:], ctx_t[bass.ds(c, 1)].rearrange("a p t d -> (a p) t d"))\
                    .then_inc(tokens_in, 16)

            def store_split(c):
                for j in range(4):
                    sp.wait_ge(proj_lo[j], c + 1)
                    sp.wait_ge(proj_hi[j], c + 1)
                    sp.dma_start(split_dram[bass.ds(c, 1), j].rearrange("a h p t -> (a p) h t"),
                                 split[:, j].bitcast(F32)).then_inc(split_stored, 16)

            def load_stack(c, h):
                for a, stack in enumerate((kstack[h], qstack[h])):
                    for head in range(2):
                        for prod in range(4):
                            part = prod % 2 if a == 0 else prod // 2
                            src = split_dram[bass.ds(c, 1), 2 * a + h, part].rearrange(
                                "a (g s d) t -> s (a d) g t", s=2, d=HD)[head]
                            row = 64 * head + HD * prod
                            dst = stack[row:row + HD, :, head, :] if a == 0 else stack[row:row + HD, :, :]
                            sp.dma_start(dst.bitcast(F32), src).then_inc(stack_loaded[h], 16)

            load_tokens(0)
            sp.dma_start(gate_rows[:], gate_w).then_inc(experts_in, 16)
            for dst, w in ((wk, w_k), (wv, w_v), (wq, w_q), (wo, w_o)):
                sp.dma_start(dst[:], w.rearrange("(k p) n -> p k n", p=P)).then_inc(weights_in, 16)
            for dst, v in ((bq, b_q), (bk, b_k)):
                for k in range(KD):
                    sp.dma_start(dst[:, k:k + 1], v.rearrange("(k p a) -> k p a", p=P, a=1)[k])\
                        .then_inc(weights_in, 16)
            for i in range(2):
                sp.dma_start(bv_all[:, i, :], on_all(b_v)).then_inc(weights_in, 16)
            sp.dma_start(bo_all[:], on_all(b_o)).then_inc(weights_in, 16)
            for i, g in enumerate((g_xattn, g_ffn)):
                sp.dma_start(gates_in[:, i:i + 1], on_all(g)).then_inc(weights_in, 16)
            for k in range(KD):
                sp.wait_ge(ctxT_filled[k], 1)
            load_tokens(1)
            store_split(0)
            sp.wait_ge(split_stored, 64)
            load_stack(0, 0)

            def iteration(b, first=False, tokens=True, prep=True):
                if not first:
                    sp.wait_ge(half_scored[1], b)
                load_stack(b, 1)
                if tokens:
                    for k in range(KD):
                        sp.wait_ge(ctxT_filled[k], b + 2)
                    load_tokens(b + 2)
                if prep:
                    store_split(b + 1)
                    sp.wait_ge(split_stored, 64 * (b + 2))
                    sp.wait_ge(half_scored[0], b + 1)
                    load_stack(b + 1, 0)

            iteration(0, first=True)
            with sp.Fori(1, B - 2) as b:
                iteration(b)
            iteration(B - 2, tokens=False)
            sp.dma_start(expert_rows, expert_w.rearrange("e (k p) h -> p (e k) h", p=P))\
                .then_inc(experts_in, 16)
            iteration(B - 1, tokens=False, prep=False)

            sp.wait_ge(plan_ready, 1)
            for e in range(E):
                at = sp.value_load(pad_row[0:1, e:e + 1], min_val=e * REGION, max_val=e * REGION + B * T)
                sp.dma_start(regions[bass.ds(at, P), :], padding[:]).then_inc(padding_stored, 16)
            sp.wait_ge(padding_stored, 16 * E)
            sp.wait_ge(regions_stored, 16 * NT + 16)
            sp.wait_ge(plan_ready, 2)

            def load_tile(i, s, first):
                at = sp.value_load(tile_row[0:1, bass.ds(SLOTS * i + s, 1)], min_val=0,
                                   max_val=E * REGION)
                if not first:
                    sp.wait_ge(row_stored[s], 16 * i)
                sp.dma_start(rows_in[:, s, :], regions[bass.ds(at, P), :]).then_inc(tile_loaded[s], 16)

            for s in range(SLOTS):
                load_tile(0, s, first=True)
            with sp.Fori(1, STEPS) as i:
                for s in range(SLOTS):
                    load_tile(i, s, first=False)
            for s in range(SLOTS):
                sp.wait_ge(row_stored[s], 16 * STEPS)

        @block.gpsimd
        def _(pool):
            nc.gpsimd.memset(identity[:], 0.0)
            nc.gpsimd.memset(identity_bf[:], 0.0)
            nc.gpsimd.memset(causal_bf[:], 0.0)
            nc.gpsimd.memset(minus_half[:], -0.5).then_inc(consts_zeroed, 1)
            pool.wait_ge(consts_zeroed, 1)
            for m in (identity, identity_bf):
                nc.gpsimd.affine_select(out=m[:], in_=m[:], compare_op=ALU.not_equal, fill=1.0, base=0,
                                        pattern=[[-1, P]], channel_multiplier=1)
            for rows, base, done in ((P, KB, consts_zeroed), (KB, 0, consts_ready)):
                last = nc.gpsimd.affine_select(out=causal_bf[0:rows], in_=causal_bf[0:rows],
                                               compare_op=ALU.is_ge, fill=NEG, base=base,
                                               pattern=[[1, KB]], channel_multiplier=-1)
                last.then_inc(done, 1)
                pool.wait_ge(done, 2 if rows == P else 1)

            nc.gpsimd.iota(ids[:], pattern=[[P, NT]], base=0, channel_multiplier=1)
            for t in range(TT):
                nc.gpsimd.iota(region_base[:, t, :], pattern=[[REGION, E]], base=0, channel_multiplier=0,
                               allow_small_or_imprecise_dtypes=True)
                nc.gpsimd.iota(first_wins[:, t, :], pattern=[[-1, E]], base=E, channel_multiplier=0,
                               allow_small_or_imprecise_dtypes=True)
            nc.gpsimd.iota(thresholds[:], pattern=[[0, E], [P, NT]], base=0, channel_multiplier=0,
                           allow_small_or_imprecise_dtypes=True)
            nc.gpsimd.iota(tile_no[:], pattern=[[1, ROUTED], [0, E]], base=0, channel_multiplier=0,
                           allow_small_or_imprecise_dtypes=True)
            nc.gpsimd.memset(padding[:], 0.0)
            nc.gpsimd.memset(upto[:], 1.0)
            nc.gpsimd.memset(earlier_bf[:], 1.0)
            nc.gpsimd.memset(seen[:], 0.0).then_inc(seen_ready, 1)
            nc.gpsimd.memset(ones_bf[:], 1.0).then_inc(consts_zeroed, 1)
            pool.wait_ge(consts_zeroed, 3)
            nc.gpsimd.iota(padding[:, ID:ID + 1].bitcast(U32), pattern=[[0, 1]], base=B * T,
                           channel_multiplier=1).then_inc(padding_ready, 1)
            nc.gpsimd.affine_select(out=upto[:], in_=upto[:], compare_op=ALU.is_ge, fill=0.0, base=0,
                                    pattern=[[1, E], [-1, E]], channel_multiplier=0)
            nc.gpsimd.affine_select(out=earlier_bf[:], in_=earlier_bf[:], compare_op=ALU.is_gt, fill=0.0,
                                    base=0, pattern=[[1, P]], channel_multiplier=-1)\
                .then_inc(consts_ready, 1)

            pool.wait_ge(padding_ready, 1)
            pool.dma_start(regions[E * REGION:E * REGION + P, :], padding[:]).then_inc(regions_stored, 16)

            def rstd_of(c):
                pool.wait_ge(ln_var_eps, c + 1)
                nc.gpsimd.tensor_tensor(rstd[:], var_eps[:], minus_half[:], ALU.pow).then_inc(ln_rstd, 1)

            def residual(c):
                pool.wait_ge(xhat_ready, c + 1)
                for t in range(TT):
                    row = x_ring[:, bass.ds(TT * (c % 4) + t, 1), :].rearrange("p a d -> p (a d)")
                    last = nc.gpsimd.tensor_tensor(row, row, bo_all[:], ALU.add)
                last.then_inc(resid_ready, 1)

            def x1_rstd_of(c):
                pool.wait_ge(x1_var_eps, c + 1)
                nc.gpsimd.tensor_tensor(x1_rows[:, :, RSTD], x1_eps[:], minus_half[:], ALU.pow)\
                    .then_inc(x1_rstd, 1)

            def scatter(c, t):
                if t == 0:
                    pool.wait_ge(padding_ready, 1)
                    pool.wait_ge(dest_ready, c + 1)
                    pool.wait_ge(x1_rstd, c + 1)
                nc.gpsimd.indirect_dma_start(
                    regions[:, :], bass.IndirectOffsetOnAxis(ap=dest[:, t:t + 1], axis=0),
                    x1_rows[:, t, :], None).then_inc(regions_stored, 16)

            def scale_v(b, blk):
                if blk < 0:
                    b, blk = b - 1, blk + BLOCKS
                pool.wait_ge(zinv_done, BLOCKS * b + blk + 1)
                if not (isinstance(b, int) and BLOCKS * b + blk < RING):
                    pool.wait_ge(pv_done, BLOCKS * b + blk - RING + 1)
                if blk == 0:
                    pool.wait_ge(v_copied[0], b + 1)
                    pool.wait_ge(v_copied[1], b + 1)
                h, kb = divmod(blk, NKB)
                slot = blk % RING
                rows = v_rows[:, bass.ds(b % 2, 1), kb, PAIRS * h:PAIRS * (h + 1), :]
                rows = rows.rearrange("p a g d -> p (a g) d")
                nc.gpsimd.tensor_tensor(v_scaled[:, slot], rows,
                                        z_inv[:, slot, :].unsqueeze(2).to_broadcast([P, PAIRS, 2 * HD]),
                                        ALU.mult).then_inc(v_scaled_done, 1)

            def iteration(b, first=False, ln=True):
                for blk in range(BLOCKS):
                    if not (first and blk < 2):
                        scale_v(b, blk - 2)
                    if blk == 2 and not (isinstance(b, int) and b == B - 1):
                        residual(b + 1)
                    if blk == 9 and not first:
                        x1_rstd_of(b - 1)
                    if blk == 13 and ln:
                        rstd_of(b + 2)
                    if blk in (14, 15) and not first:
                        for t in range(2):
                            scatter(b - 1, 2 * (blk - 14) + t)

            pool.wait_ge(wo_scaled, 1)
            rstd_of(0)
            residual(0)
            rstd_of(1)
            iteration(0, first=True)
            with pool.Fori(1, B - 2) as b:
                iteration(b)
            iteration(B - 2, ln=False)
            iteration(B - 1, ln=False)
            scale_v(B, -2)
            scale_v(B, -1)
            x1_rstd_of(B - 1)
            for t in range(TT):
                scatter(B - 1, t)

            def store_tile(count, s):
                pool.wait_ge(padding_ready, 1)
                pool.wait_ge(row_ready[s], count)
                nc.gpsimd.indirect_dma_start(
                    out_rows, bass.IndirectOffsetOnAxis(ap=rows_in[:, s, ID:ID + 1].bitcast(U32), axis=0),
                    rows_in[:, s, 0:D], None, bounds_check=last_id, oob_is_err=False)\
                    .then_inc(row_stored[s], 16)

            last_id = nc.gpsimd.to_reg(B * T - 1)
            with pool.Fori(1, STEPS + 1) as count:
                for s in range(SLOTS):
                    store_tile(count, s)

        @block.tensor
        def _(pe):
            def transpose_ctx(c, k):
                if k == 0:
                    pe.wait_ge(tokens_in, 32 * (c + 1))
                if not (isinstance(c, int) and c == 0):
                    pe.wait_ge(v_copied[k], c)
                for t in range(TT):
                    last = nc.tensor.transpose(misc_ps[:, k, P * t:P * (t + 1)],
                                               ctx_in[:, t, P * k:P * (k + 1)], identity[:])
                last.then_inc(ctxT_filled[k], 1)

            def transpose_xhat(c, k):
                if k == 0:
                    pe.wait_ge(xhat_ready, c + 1)
                pe.wait_ge(proj_lo[k], c + 1)
                for t in range(TT):
                    last = nc.tensor.transpose(misc_ps[:, k, P * t:P * (t + 1)],
                                               xhat[:, t, P * k:P * (k + 1)], identity[:])
                last.then_inc(xhatT_filled[k], 1)

            def project(c, j):
                a, m = PROJ[j]
                src, w = (ctxT, wk) if a == "k" else (xhatT, wq)
                for k in range(KD):
                    pe.wait_ge(ctxT_copied[k] if a == "k" else xhatT_copied[k], c + 1)
                for k in range(KD):
                    last = nc.tensor.matmul(misc_ps[:, m, :], w[:, k, P * m:P * (m + 1)], src[:, k, :],
                                            start=(k == 0), stop=(k == KD - 1))
                last.then_inc(proj_filled[j], 1)

            def project_v(c, i, post):
                if post:
                    pe.wait_ge((logits_read, rank_read)[i], c - 1)
                else:
                    pe.wait_ge(proj_lo[2 + i], c + 1)
                for t in range(2):
                    cols = slice(P * (2 * i + t), P * (2 * i + t + 1))
                    for k in range(KD):
                        last = nc.tensor.matmul(misc_ps[:, i, D * t:D * (t + 1)], ctxT[:, k, cols],
                                                wv[:, k, :], start=(k == 0), stop=(k == KD - 1))
                last.then_inc(v_filled[i], 1)

            def project_out(c, i, bank_free, count):
                pe.wait_ge(bank_free, count)
                for h in range(KD):
                    pe.wait_ge(attn_copied[h], c + 1)
                for t in range(2):
                    cols = slice(P * (2 * i + t), P * (2 * i + t + 1))
                    for h in range(KD):
                        last = nc.tensor.matmul(misc_ps[:, i, D * t:D * (t + 1)], attnT[:, h, cols],
                                                wo[:, h, :], start=(h == 0), stop=(h == KD - 1))
                last.then_inc(y_filled[i], 1)

            def keys_of(h, g, kb):
                return kstack[h][:, g].rearrange("p s (i kb) -> p (s i) kb", kb=NKB)[:, :, kb]

            def transpose_x1(c, k):
                pe.wait_ge(y_added[0], c + 1)
                pe.wait_ge(y_added[1], c + 1)
                for t in range(TT):
                    last = nc.tensor.transpose(misc_ps[:, k, P * t:P * (t + 1)],
                                               x1_rows[:, t, P * k:P * (k + 1)], identity[:])
                last.then_inc(x1T_filled[k], 1)

            def gate_logits(c):
                pe.wait_ge(x1T_copied[0], c + 1)
                pe.wait_ge(x1T_copied[1], c + 1)
                for t in range(TT):
                    for k in range(KD):
                        last = nc.tensor.matmul(misc_ps[:, 0, E * t:E * (t + 1)],
                                                x1T[:, k, P * t:P * (t + 1)], gateT[:, k, :],
                                                start=(k == 0), stop=(k == KD - 1))
                last.then_inc(logits_filled, 1)

            def ranks(c):
                pe.wait_ge(onehot_ready, c + 1)
                pe.wait_ge(seen_ready, c + 1)
                out_all = misc_ps[:, 1, 0:TT * E]
                nc.tensor.matmul(out_all, earlier_bf[:], onehot[:].rearrange("p t e -> p (t e)"),
                                 start=True, stop=False)
                nc.tensor.matmul(out_all.rearrange("p (t e) -> p t e", t=TT), ones_bf[:],
                                 seen[:].unsqueeze(1).to_broadcast([P, TT, E]), start=False, stop=False)
                for t in range(TT - 1):
                    after = TT - 1 - t
                    last = nc.tensor.matmul(
                        misc_ps[:, 1, E * (t + 1):E * TT].rearrange("p (t e) -> p t e", t=after),
                        ones_bf[:], onehot[:, t:t + 1, :].to_broadcast([P, after, E]),
                        start=False, stop=(t == TT - 2))
                last.then_inc(rank_filled, 1)

            def transpose_expert(e):
                for k in range(KD):
                    for f in range(KD):
                        last = nc.tensor.transpose(
                            misc_ps[:, e % 2, D * k + P * f:D * k + P * (f + 1)],
                            expert_rows[:, KD * e + f, P * k:P * (k + 1)], identity[:])
                last.then_inc(expertT_filled, 1)

            def score(b, n, first):
                blk, g = divmod(n, PAIRS)
                h, kb = divmod(blk, NKB)
                L = queries(kb)
                if kb == 0 and g == 0:
                    pe.wait_ge(stack_loaded[h], 16 * STACK_DMAS * (b + 1))
                if not (first and n < BANKS):
                    pe.wait_ge(exp_done, TILES * b + n - BANKS + 1)
                s = scores_ps[:, n % BANKS, :]
                product = nc.tensor.matmul(s[:, 0:L], keys_of(h, g, kb),
                                           qstack[h][:, g, KB * kb:T], start=True, stop=False)
                if n % (NKB * PAIRS) == NKB * PAIRS - 1:
                    product.then_inc(half_scored[h], 1)
                nc.tensor.matmul(s[:, 0:KB], identity_bf[:], causal_bf[:], start=False, stop=True)\
                    .then_inc(scores_done, 1)

            def times_v(b, blk, first=False):
                if blk < 0:
                    b, blk = b - 1, blk + BLOCKS
                h, kb = divmod(blk, NKB)
                if kb == 0 and not first:
                    pe.wait_ge(attn_copied[h], b)
                pe.wait_ge(v_scaled_done, BLOCKS * b + blk + 1)
                slot = blk % RING
                for g in range(PAIRS):
                    last = nc.tensor.matmul(attn_ps[32 * g:32 * (g + 1), h, KB * kb:T],
                                            v_scaled[:, slot, g, :], probs[:, slot, g, 0:queries(kb)],
                                            start=(kb == 0), stop=(kb == NKB - 1))
                last.then_inc(pv_done, 1)

            def prepare(c, n, post=True):
                if n == 0:
                    transpose_ctx(c, 0)
                if n == 1:
                    transpose_ctx(c, 1)
                if n == 4:
                    project(c, 0)
                if n == 7:
                    project(c, 1)
                if n == 10:
                    transpose_xhat(c, 0)
                if n == 12:
                    transpose_xhat(c, 1)
                if n == 15:
                    project(c, 2)
                if n == 19:
                    project(c, 3)
                if n == 42:
                    project_v(c, 0, post)
                if n == 46:
                    project_v(c, 1, post)

            def finish(c, n, prep=True):
                if n in (23, 25):
                    i = (n - 23) // 2
                    if prep:
                        project_out(c, i, proj_lo[2 + i], c + 3)
                    else:
                        project_out(c, i, v_copied[i], c + 2)
                if n == 29:
                    transpose_x1(c, 0)
                if n == 31:
                    transpose_x1(c, 1)
                if n == 34:
                    gate_logits(c)
                if n == 40:
                    ranks(c)

            def iteration(b, first=False, prep=True):
                for n in range(TILES):
                    score(b, n, first)
                    if n % PAIRS == 0 and not (first and n < LAG * PAIRS):
                        times_v(b, n // PAIRS - LAG, first)
                    if not first:
                        finish(b - 1, n, prep)
                    if prep:
                        prepare(b + 1, n, post=not first)
                    elif n in range(46, 62, 2):
                        e = (n - 46) // 2
                        if e == 0:
                            pe.wait_ge(experts_in, 32)
                            pe.wait_ge(logits_read, B - 1)
                        elif e == 1:
                            pe.wait_ge(rank_read, B - 1)
                        else:
                            pe.wait_ge(expertT_copied, e - 1)
                        transpose_expert(e)

            pe.wait_ge(consts_ready, 1)
            pe.wait_ge(gate_centred, 1)
            for k in range(KD):
                last = nc.tensor.transpose(attn_ps[:, 0, E * k:E * (k + 1)],
                                           gate_rows[:, P * k:P * (k + 1)], identity[0:E, 0:E])
            last.then_inc(gateT_filled, 1)
            for n in range(TILES):
                if n == 4:
                    pe.wait_ge(weights_in, 16 * WEIGHT_DMAS)
                    pe.wait_ge(wq_scaled, 2)
                prepare(0, n, post=False)
            pe.wait_ge(zeros_ready, 1)
            pe.wait_ge(gateT_copied, 1)
            pe.wait_ge(consts_ready, 2)
            iteration(0, first=True)
            with pe.Fori(1, B - 1) as b:
                iteration(b)
            iteration(B - 1, prep=False)
            for blk in range(-LAG, 0):
                times_v(B, blk)
            for i in range(2):
                project_out(B - 1, i, expertT_copied, E - 1 + i)
            for k in range(KD):
                transpose_x1(B - 1, k)
            gate_logits(B - 1)
            ranks(B - 1)
            pe.wait_ge(seen_ready, B + 1)
            nc.tensor.matmul(attn_ps[:, 0, 0:E], ones_bf[:], seen[:], start=True, stop=True)\
                .then_inc(counts_filled, 1)

            def transpose_h(i, s):
                pe.wait_ge(h_ready[s], i + 1)
                for k in range(KD):
                    last = nc.tensor.transpose(hT_banks[s % 4][:, P * k:P * (k + 1)],
                                               h_rows[:, s, P * k:P * (k + 1)], identity[:])
                last.then_inc(hT_filled[s], 1)

            def times_expert(i, s, first):
                e = pe.value_load(tile_expert[0:1, bass.ds(SLOTS * i + s, 1)], min_val=0, max_val=E - 1)
                pe.wait_ge(hT_copied[s], i + 1)
                if s >= 4:
                    pe.wait_ge(expert_read[s - 4], i + 1)
                elif not first:
                    pe.wait_ge(expert_read[s + 4], i)
                for k in range(KD):
                    last = nc.tensor.matmul(expert_banks[s % 4], hT[:, s % 4, k, :],
                                            expertT[:, k, bass.ds(e, 1), :].rearrange("p a f -> p (a f)"),
                                            start=(k == 0), stop=(k == KD - 1))
                last.then_inc(expert_filled[s], 1)

            pe.wait_ge(plan_ready, 2)
            transpose_h(0, 0)

            def step(i, first=False, last=False):
                for s in range(SLOTS):
                    if s < SLOTS - 1:
                        transpose_h(i, s + 1)
                    elif not last:
                        transpose_h(i + 1, 0)
                    times_expert(i, s, first)

            step(0, first=True)
            with pe.Fori(1, STEPS - 1) as i:
                step(i)
            step(STEPS - 1, last=True)

        @block.scalar
        def _(act):
            act.wait_ge(gateT_filled, 1)
            nc.scalar.copy(gateT[:].rearrange("p k e -> p (k e)"), attn_ps[:, 0, 0:KD * E])\
                .then_inc(gateT_copied, 1)
            act.wait_ge(weights_in, 16 * WEIGHT_DMAS)
            nc.scalar.activation(gates[:], gates_in[:], ACT.Tanh).then_inc(gates_ready, 1)
            nc.scalar.mul(wq[:], wq[:], SCALE).then_inc(wq_scaled, 1)
            nc.scalar.mul(bq[:], bq[:], SCALE).then_inc(wq_scaled, 1)
            act.wait_ge(wq_scaled, 2)

            def copy(dst, src, filled, count, copied):
                act.wait_ge(filled, count)
                nc.scalar.copy(dst, src).then_inc(copied, 1)

            def split_hi(c, j):
                a, m = PROJ[j]
                act.wait_ge(proj_filled[j], c + 1)
                if not (isinstance(c, int) and c == 0):
                    act.wait_ge(split_stored, 64 * c)
                nc.scalar.activation(split_order(split[:, j, 0, :], j), natural(misc_ps[:, m, :]),
                                     ACT.Identity,
                                     bias=(bk if a == "k" else bq)[:, m:m + 1]).then_inc(proj_hi[j], 1)

            def copy_attn(b, h):
                act.wait_ge(pv_done, BLOCKS * b + NKB * (h + 1))
                nc.scalar.copy(attnT[:, h, :], attn_ps[:, h, :]).then_inc(attn_copied[h], 1)

            def exps(b, n, first):
                blk, g = divmod(n, PAIRS)
                slot = blk % RING
                act.wait_ge(max_done, TILES * b + n + 1)
                if g == 0 and not (first and blk < RING):
                    act.wait_ge(pv_done, BLOCKS * b + blk - RING + 1)
                L = queries(blk % NKB)
                nc.scalar.activation(probs[:, slot, g, 0:L], scores_ps[:, n % BANKS, 0:L], ACT.Exp,
                                     bias=neg_max[:, slot, g:g + 1],
                                     accum_out=z_sum[:, slot, g:g + 1]).then_inc(exp_done, 1)

            def prepare(c, n):
                if n == 2:
                    if not (isinstance(c, int) and c == 0):
                        act.wait_ge(v_filled[1], c)
                    copy(ctxT[:, 0, :], misc_ps[:, 0, :], ctxT_filled[0], c + 1, ctxT_copied[0])
                if n == 6:
                    split_hi(c, 0)
                if n == 9:
                    split_hi(c, 1)
                if n == 12:
                    if not (isinstance(c, int) and c == 0):
                        act.wait_ge(proj_filled[3], c)
                    copy(xhatT[:, 0, :], misc_ps[:, 0, :], xhatT_filled[0], c + 1, xhatT_copied[0])
                if n == 17:
                    split_hi(c, 2)
                if n == 21:
                    split_hi(c, 3)

            def copy_x1T(c, k):
                copy(x1T[:, k, :], misc_ps[:, k, :], x1T_filled[k], c + 1, x1T_copied[k])

            def copy_expert(e):
                act.wait_ge(expertT_filled, e + 1)
                nc.scalar.activation(expertT[:, :, e, :],
                                     misc_ps[:, e % 2, :].rearrange("p (k f) -> p k f", k=KD), ACT.Copy,
                                     scale=gates[:, 1:2]).then_inc(expertT_copied, 1)

            def iteration(b, first=False, last=False):
                for n in range(TILES):
                    if not last:
                        prepare(b + 1, n)
                    elif n in range(48, 64, 2):
                        copy_expert((n - 48) // 2)
                    if n == 14 and not first:
                        copy_attn(b - 1, 1)
                    if n in (31, 33) and not first:
                        copy_x1T(b - 1, (n - 31) // 2)
                    if n == 43:
                        copy_attn(b, 0)
                    exps(b, n, first)

            for n in range(TILES):
                prepare(0, n)
            iteration(0, first=True)
            with act.Fori(1, B - 1) as b:
                iteration(b)
            iteration(B - 1, last=True)
            copy_attn(B - 1, 1)
            for k in range(KD):
                copy_x1T(B - 1, k)

            with act.Fori(0, STEPS) as i:
                for s in range(SLOTS):
                    copy(hT[:, s % 4].rearrange("p k t -> p (k t)"), hT_banks[s % 4], hT_filled[s], i + 1,
                         hT_copied[s])

        @block.vector
        def _(dve):
            for h in range(KD):
                nc.vector.memset(kstack[h][0:64, :, 1, :].bitcast(F32), 0.0)
                nc.vector.memset(kstack[h][64:128, :, 0, :].bitcast(F32), 0.0)
            nc.vector.memset(v_rows[:], 0.0).then_inc(zeros_ready, 1)
            dve.wait_ge(experts_in, 16)
            nc.vector.reduce_sum(gate_mean[:], gate_rows[:], AX_X).then_inc(gate_step, 1)
            dve.wait_ge(gate_step, 1)
            nc.vector.tensor_scalar(gate_mean[:], gate_mean[:], 1.0 / D, None, ALU.mult)\
                .then_inc(gate_step, 1)
            dve.wait_ge(gate_step, 2)
            nc.vector.tensor_scalar(gate_rows[:], gate_rows[:], gate_mean[:], None, ALU.subtract)\
                .then_inc(gate_centred, 1)
            dve.wait_ge(gates_ready, 1)
            nc.vector.tensor_scalar(wo[:], wo[:], gates[:, 0:1], None, ALU.mult)
            nc.vector.tensor_scalar(bo_all[:], bo_all[:], gates[:, 0:1], None, ALU.mult)\
                .then_inc(wo_scaled, 1)

            def tile_stats(c, t, row):
                nc.vector.bn_stats(stats[:, t, :], row)

            def split_lo(c, j):
                a, m = PROJ[j]
                dve.wait_ge(proj_hi[j], c + 1)
                nc.vector.scalar_tensor_tensor(
                    split_order(split[:, j, 1, :], j), natural(misc_ps[:, m, :]),
                    (bk if a == "k" else bq)[:, m:m + 1],
                    split_order(split[:, j, 0, :], j).bitcast(F32), ALU.add, ALU.subtract).then_inc(proj_lo[j], 1)

            def copy_v(c, i):
                dve.wait_ge(v_filled[i], c + 1)
                for s in range(2):
                    for head in range(2):
                        dst = v_rows[64 * head:64 * (head + 1), bass.ds(c % 2, 1),
                                     4 * i + s:4 * i + s + 3:2, :, HD * head:HD * (head + 1)]
                        src = misc_ps[64 * s:64 * (s + 1), i, :].rearrange(
                            "p (t g s d) -> p s t g d", t=2, s=2, d=HD)[:, head]
                        bias = bv_all[64 * s:64 * (s + 1)].rearrange(
                            "p t (g s d) -> p s t g d", s=2, d=HD)[:, head]
                        last = nc.vector.tensor_tensor(dst.rearrange("p a t g d -> p (a t) g d"), src,
                                                       bias, ALU.add)
                last.then_inc(v_copied[i], 1)

            def add_y(b, i):
                dve.wait_ge(y_filled[i], b + 1)
                if i == 0:
                    dve.wait_ge(resid_ready, b + 1)
                    dve.wait_ge(regions_stored, 16 * TT * b + 16)
                nc.vector.tensor_tensor(x1_rows[:, 2 * i:2 * i + 2, 0:D],
                                        misc_ps[:, i, :].rearrange("p (t d) -> p t d", t=2),
                                        x_ring[:, bass.ds(TT * (b % 4) + 2 * i, 2), :], ALU.add)\
                    .then_inc(y_added[i], 1)

            def after(c, k):
                dve.wait_ge(route, ROUTE_STEPS * c + k)

            def finish(c, n):
                if n in (25, 27):
                    add_y(c, (n - 25) // 2)
                if 28 <= n < 28 + TT:
                    t = n - 28
                    if t == 0:
                        dve.wait_ge(y_added[0], c + 1)
                        dve.wait_ge(y_added[1], c + 1)
                        nc.vector.tensor_copy(x1_rows[:, :, ID].bitcast(U32),
                                              ids[:, bass.ds(TT * c, TT)])
                    last = nc.vector.bn_stats(x1_bn[:, t, :], x1_rows[:, t, 0:D])
                    if t == TT - 1:
                        last.then_inc(x1_stats, 1)
                logits = misc_ps[:, 0, 0:TT * E].rearrange("p (t e) -> p t e", t=TT)
                rank = misc_ps[:, 1, 0:TT * E].rearrange("p (t e) -> p t e", t=TT)

                def over_experts(v):
                    return v.unsqueeze(2).to_broadcast([P, TT, E])

                if n == 36:
                    dve.wait_ge(logits_filled, c + 1)
                    dve.wait_ge(x1_stats, c + 1)
                    nc.vector.reduce_max(best[:], logits, AX_X).then_inc(route, 1)
                    for t in range(TT):
                        last = nc.vector.bn_aggr(x1_rows[:, t, MEAN:VAR + 1], x1_bn[:, t, :])
                    last.then_inc(x1_mean_var, 1)
                if n == 37:
                    after(c, 1)
                    nc.vector.tensor_tensor(ranked[:], logits, over_experts(best[:]), ALU.is_equal)\
                        .then_inc(logits_read, 1)
                    dve.wait_ge(x1_mean_var, c + 1)
                    nc.vector.tensor_scalar(x1_eps[:], x1_rows[:, :, VAR], EPS, None, ALU.add)\
                        .then_inc(x1_var_eps, 1)
                    dve.wait_ge(logits_read, c + 1)
                    nc.vector.tensor_tensor(ranked[:], ranked[:], first_wins[:], ALU.mult)\
                        .then_inc(route, 1)
                if n == 38:
                    after(c, 2)
                    nc.vector.reduce_max(top_rank[:], ranked[:], AX_X).then_inc(route, 1)
                if n == 39:
                    after(c, 3)
                    nc.vector.tensor_tensor(onehot[:], ranked[:], over_experts(top_rank[:]), ALU.is_equal)\
                        .then_inc(onehot_ready, 1)
                if n == 42:
                    dve.wait_ge(rank_filled, c + 1)
                    nc.vector.tensor_tensor(place[:], rank, region_base[:], ALU.add)\
                        .then_inc(rank_read, 1)
                    with nc.allow_low_precision(reason="counts up to NT, exact in bfloat16"):
                        nc.vector.reduce_sum(batch_seen[:], onehot[:].rearrange("p t e -> p e t"), AX_X)\
                            .then_inc(route, 1)
                if n == 43:
                    dve.wait_ge(rank_read, c + 1)
                    nc.vector.tensor_tensor(place[:], place[:], onehot[:], ALU.mult).then_inc(route, 1)
                if n == 44:
                    after(c, 5)
                    nc.vector.reduce_sum(dest_f[:], place[:], AX_X).then_inc(route, 1)
                    nc.vector.tensor_tensor(seen[:], seen[:], batch_seen[:], ALU.add)\
                        .then_inc(seen_ready, 1)
                if n == 45:
                    after(c, 6)
                    nc.vector.tensor_copy(dest[:], dest_f[:]).then_inc(dest_ready, 1)

            def maxes(b, n, first):
                blk, g = divmod(n, PAIRS)
                dve.wait_ge(scores_done, TILES * b + n + 1)
                nc.vector.tensor_reduce(neg_max[:, blk % RING, g:g + 1],
                                        scores_ps[:, n % BANKS, 0:queries(blk % NKB)], AX_X, ALU.max,
                                        negate=True).then_inc(max_done, 1)

            def invert_z(b, blk):
                if blk < 0:
                    b, blk = b - 1, blk + BLOCKS
                dve.wait_ge(exp_done, TILES * b + PAIRS * (blk + 1))
                nc.vector.reciprocal(z_inv[:, blk % RING, :], z_sum[:, blk % RING, :])\
                    .then_inc(zinv_done, 1)

            def layernorm(c, n):
                if n < TT:
                    if n == 0:
                        dve.wait_ge(tokens_in, 32 * (c + 1))
                    row = x_ring[:, bass.ds(TT * (c % 4) + n, 1), :].rearrange("p a d -> p (a d)")
                    last = nc.vector.bn_stats(stats[:, n, :], row)
                    if n == TT - 1:
                        last.then_inc(ln_stats, 1)
                if n == 5:
                    dve.wait_ge(ln_stats, c + 1)
                    nc.vector.memset(ln_fence[:], 0.0)
                    for t in range(TT):
                        last = nc.vector.bn_aggr(mean_var[:, t, :], stats[:, t, :])
                    last.then_inc(ln_mean_var, 1)
                if n == 6:
                    dve.wait_ge(ln_mean_var, c + 1)
                    nc.vector.tensor_scalar(var_eps[:], mean_var[:, :, 1], EPS, None, ALU.add)\
                        .then_inc(ln_var_eps, 1)
                if 11 <= n < 11 + TT:
                    t = n - 11
                    if t == 0:
                        dve.wait_ge(ln_rstd, c + 1)
                        if not (isinstance(c, int) and c == 0):
                            dve.wait_ge(xhatT_filled[1], c)
                    row = x_ring[:, bass.ds(TT * (c % 4) + t, 1), :].rearrange("p a d -> p (a d)")
                    last = nc.vector.tensor_scalar(xhat[:, t, :], row, mean_var[:, t, 0:1],
                                                   rstd[:, t:t + 1], ALU.subtract, ALU.mult)
                    if t == TT - 1:
                        last.then_inc(xhat_ready, 1)

            def prepare(c, n):
                if n == 3:
                    if not (isinstance(c, int) and c == 0):
                        dve.wait_ge(v_filled[1], c)
                    dve.wait_ge(ctxT_filled[1], c + 1)
                    nc.vector.tensor_copy(ctxT[:, 1, :], misc_ps[:, 1, :]).then_inc(ctxT_copied[1], 1)
                if n == 8:
                    split_lo(c, 0)
                if n == 11:
                    split_lo(c, 1)
                if n == 14:
                    dve.wait_ge(xhatT_filled[1], c + 1)
                    if not (isinstance(c, int) and c == 0):
                        dve.wait_ge(proj_filled[3], c)
                    nc.vector.tensor_copy(xhatT[:, 1, :], misc_ps[:, 1, :]).then_inc(xhatT_copied[1], 1)
                if n == 19:
                    split_lo(c, 2)
                if n == 23:
                    split_lo(c, 3)
                if n == 46:
                    copy_v(c, 0)
                if n == 50:
                    copy_v(c, 1)

            def iteration(b, first=False, ln=True, prep=True):
                for n in range(TILES):
                    if prep:
                        prepare(b + 1, n)
                    if not first:
                        finish(b - 1, n)
                    if ln and n >= 47:
                        layernorm(b + 2, n - 47)
                    if n % PAIRS == 0 and not (first and n < 2 * PAIRS):
                        invert_z(b, n // PAIRS - 2)
                    maxes(b, n, first)

            for n in range(16):
                layernorm(0, n)
            for n in range(TILES):
                if n == 46:
                    dve.wait_ge(zeros_ready, 1)
                prepare(0, n)
            for n in range(16):
                layernorm(1, n)
            dve.wait_ge(consts_ready, 2)
            iteration(0, first=True)
            with dve.Fori(1, B - 2) as b:
                iteration(b)
            iteration(B - 2, ln=False)
            iteration(B - 1, ln=False, prep=False)
            invert_z(B, -2)
            invert_z(B, -1)
            for n in range(TILES):
                finish(B - 1, n)

            steps = [0]

            def then(instruction):
                steps[0] += 1
                instruction.then_inc(plan, 1)
                dve.wait_ge(plan, steps[0])

            def over_tiles(v):
                return v.unsqueeze(1).to_broadcast([1, ROUTED, E])

            dve.wait_ge(counts_filled, 1)
            counts = attn_ps[0:1, 0, 0:E]
            nc.vector.tensor_tensor(pad_row[:], counts, region_base[0:1, 0, :], ALU.add)\
                .then_inc(plan_ready, 1)
            then(nc.vector.tensor_tensor(past[:], counts.unsqueeze(2).to_broadcast([1, E, NT]),
                                         thresholds[:], ALU.is_gt))
            then(nc.vector.reduce_sum(tiles_of[:], past[:], AX_X))
            then(nc.vector.tensor_tensor(tiles_upto[:], tiles_of[:].unsqueeze(1).to_broadcast([1, E, E]),
                                         upto[:], ALU.mult))
            then(nc.vector.reduce_sum(ends[:], tiles_upto[:], AX_X))
            then(nc.vector.tensor_tensor(ended[:], tile_no[:], over_tiles(ends[:]), ALU.is_ge))
            nc.vector.tensor_tensor(ended_tiles[:], ended[:], over_tiles(tiles_of[:]), ALU.mult)
            then(nc.vector.reduce_sum(expert_f[:], ended[:], AX_X))
            then(nc.vector.reduce_sum(first_tile[:], ended_tiles[:], AX_X))
            then(nc.vector.tensor_tensor(in_region[:], tile_no[:, :, 0], first_tile[:], ALU.subtract))
            then(nc.vector.scalar_tensor_tensor(in_region[:], expert_f[:], float(E), in_region[:],
                                                ALU.is_lt, ALU.mult))
            then(nc.vector.scalar_tensor_tensor(row_f[:], expert_f[:], float(REGION // P), in_region[:],
                                                ALU.mult, ALU.add))
            nc.vector.tensor_scalar(tile_expert[:], expert_f[:], float(E - 1), None, ALU.min)
            nc.vector.tensor_scalar(tile_row[:], row_f[:], float(P), None, ALU.mult)\
                .then_inc(plan_ready, 1)

            def normalise(i, s):
                dve.wait_ge(tile_loaded[s], 16 * (i + 1))
                nc.vector.tensor_scalar(h_rows[:, s, :], rows_in[:, s, 0:D], rows_in[:, s, MEAN:MEAN + 1],
                                        rows_in[:, s, RSTD:RSTD + 1], ALU.subtract, ALU.mult)\
                    .then_inc(h_ready[s], 1)

            def weigh(i, s):
                dve.wait_ge(expert_filled[s], i + 1)
                nc.vector.scalar_tensor_tensor(h_rows[:, s, :], h_rows[:, s, :], gates[:, 1:2],
                                               expert_banks[s % 4], ALU.mult, ALU.add)\
                    .then_inc(expert_read[s], 1)

            def add_rows(i, s):
                dve.wait_ge(expert_read[s], i + 1)
                nc.vector.tensor_tensor(rows_in[:, s, 0:D], rows_in[:, s, 0:D], h_rows[:, s, :], ALU.add)\
                    .then_inc(row_ready[s], 1)

            def step(i, last=False):
                for s in range(SLOTS):
                    weigh(i, s)
                    if s < SLOTS - 3:
                        normalise(i, s + 3)
                    elif not last:
                        normalise(i + 1, s + 3 - SLOTS)
                    add_rows(i, s)

            for s in range(3):
                normalise(0, s)
            with dve.Fori(0, STEPS - 1) as i:
                step(i)
            step(STEPS - 1, last=True)


_INS = ["x", "ctx_1024", "g_xattn", "g_ffn", "L0_xattn_w_q", "L0_xattn_b_q", "L0_xattn_w_k",
        "L0_xattn_b_k", "L0_xattn_w_v", "L0_xattn_b_v", "L0_xattn_w_o", "L0_xattn_b_o",
        "L0_ffn_gate_w", "L0_ffn_expert_w"]


def kernel(**inputs):
    import numpy as _np
    import concourse.bacc as _bacc
    from concourse import mybir as _mybir
    from concourse.bass_utils import run_bass_kernel_spmd as _run

    nc = _bacc.Bacc("TRN2", target_bir_lowering=False, num_devices=1)
    arrays, args = {}, []
    for name in _INS:
        a = _np.ascontiguousarray(inputs[name])
        arrays[f"in_{name}"] = a
        args.append(nc.dram_tensor(f"in_{name}", a.shape, _mybir.dt.from_np(a.dtype),
                                   kind="ExternalInput").ap())
    shape = tuple(inputs["x"].shape)
    args.append(nc.dram_tensor("out_x", shape, _mybir.dt.float32, kind="ExternalOutput").ap())
    attention_moe_kernel(nc, *args)
    r = _run(nc, [arrays], core_ids=[0])
    return r.results[0]["out_x"]
```

```python
from contextlib import ExitStack

import concourse.bass as bass
from concourse import mybir

ALU = mybir.AluOpType
ACT = mybir.ActivationFunctionType
F32 = mybir.dt.float32
F32R = mybir.dt.float32r
BF16 = mybir.dt.bfloat16
I32 = mybir.dt.int32
U32 = mybir.dt.uint32
AX_X = mybir.AxisListType.X

P = 128
EPS = 1e-5
NEG = -1e30


def bank_uses(short, pairs, banks):
    use, at = [], 0
    for is_short in short:
        for g in range(pairs):
            use.append(at)
            at += 1 if not is_short or g % 2 else 0
    last = {u: n for n, u in enumerate(use)}
    before = [last[u - banks] if u >= banks else last[at + u - banks] - len(use) for u in use]
    assert at % banks == 0
    return [u % banks for u in use], before


def attention_moe_kernel(nc, x, ctx, g_xattn, g_ffn, w_q, b_q, w_k, b_k, w_v, b_v, w_o, b_o,
                         gate_w, expert_w, out):
    B, T, D = x.shape
    E = gate_w.shape[0]
    HD = 16
    KD = D // P
    TT = T // P
    NT = B * TT
    PAIRS = P // (2 * HD)
    KB = 64
    NKB = T // KB
    TILES = KD * NKB * PAIRS
    BLOCKS = KD * NKB
    BANKS = 4
    RING = 4
    LAG = 3
    SCALE = HD ** -0.5
    STACK_DMAS = 2 * 2 * 4
    assert SCALE == 0.25 and KD == 2 and NKB == 8 and TT == 4 and E == 8 and B >= 3
    ROW = D + 4
    ID, MEAN, VAR, RSTD = D, D + 1, D + 2, D + 3
    SHIFT = MEAN
    REGION = B * T + P
    EARLY = NT - TT - (E - 1)
    LATE = TT + 2 * (E - 1)
    ROUTED = EARLY + LATE
    SLOTS = EARLY
    H_SLOTS, HT_SLOTS = 10, 3
    LOADS = 12
    GROUP = 3
    assert LATE <= EARLY and EARLY % GROUP == 0 and LATE % GROUP == 0
    GC = P // TT
    ROUTE_STEPS = 6
    KEY_BLOCKS = 0, 7, 2, 4, 1, 5, 3, 6

    SHORT = [T - KB * kb <= T // 2 for _ in range(KD) for kb in KEY_BLOCKS]
    BANK_OF, READ_BEFORE = bank_uses(SHORT, PAIRS, BANKS)

    AT_CTX = 0, 1
    AT_PROJ = (3, 9), (13, 17), (33, 35), (41, 45)
    AT_XHAT = 26, 25
    AT_V = (49, 53), (57, 61)
    AT_Y = (16, 21), (19, 21)
    AT_X1T = 31, 32
    AT_GATE, AT_LOGITS, AT_RANK = 38, 45, 52
    AT_ATTN = 43, 11
    AT_X_STATS = 9, 11, 16, 17
    AT_X_VAR = 24, 29
    AT_X1_STATS = 25, 26, 27, 31
    AT_X1_VAR = 35, 36
    ENDING = ("out", "x1T", 0, "gate", 1, "logits", 2, 3, "ranks", 4, 5, "counts", 6, "sums", 7,
              "experts", 8, "rows") + tuple(range(9, ROUTED))
    AT_PAD = 6, 7, 8, 9
    BEFORE_PAD = 15
    LO_LATER = 4
    AT_ONCE = 2
    AT_PV = 3
    AT_Z = 0
    Z_LAG = 2
    AT_RESIDUAL = 1, 2
    AT_RSTD = 6
    AT_CENTRE = 6, 7
    AT_NORMALISE = 9, 10
    AT_X1_RSTD = 10
    AT_SCATTER = 14, 15
    AT_IDENTITY = 8, 10
    AT_COUNT = 61
    AT_EXPERT = 25, 28, 33, 37, 43, 48, 55, 61
    EXPERT_BANK = 1, 0, 0, 0, 0, 1, 1, 1
    PROJ_BANK = 0, 1, 0, 0
    PROJ = ("k", 0), ("k", 1), ("q", 0), ("q", 1)

    def queries(kb):
        return T - KB * kb

    def natural(v):
        return v.rearrange("p (kb i) -> p kb i", i=KB)

    def split_order(v, j):
        if PROJ[j][0] == "k":
            return v.rearrange("p (i kb) -> p kb i", kb=NKB)
        return natural(v)

    with ExitStack() as es:
        def score_columns(n, width):
            half = T // 2 * (n % 2) if SHORT[n // PAIRS] else 0
            return scores_ps[:, BANK_OF[n], half:half + width]

        def sb(name, shape, dt=F32):
            return es.enter_context(nc.sbuf_tensor(name, shape, dt))

        def sem(name):
            return es.enter_context(nc.semaphore(name))

        x_ring = sb("x_ring", [P, 4 * TT, D])
        ctx_in = sb("ctx_in", [P, TT, D])
        xhat = sb("xhat", [P, TT, D])
        ctxT = sb("ctxT", [P, KD, T])
        xhatT = sb("xhatT", [P, KD, T])
        split = sb("split", [P, 4, 2, T], F32R)
        kstack = [sb(f"kstack{h}", [P, PAIRS, 2, T], F32R) for h in range(KD)]
        qstack = [sb(f"qstack{h}", [P, PAIRS, T], F32R) for h in range(KD)]
        v_rows = sb("v_rows", [P, 2, NKB, 2 * PAIRS, 2 * HD])
        v_scaled = sb("v_scaled", [P, RING, PAIRS, 2 * HD])
        probs = sb("probs", [P, RING, PAIRS, T])
        neg_max = sb("neg_max", [P, RING, PAIRS])
        z_sum = sb("z_sum", [P, RING, PAIRS])
        z_inv = sb("z_inv", [P, RING, PAIRS])
        attnT = sb("attnT", [P, KD, T])
        wq = sb("wq", [P, KD, D])
        wk = sb("wk", [P, KD, D])
        wv = sb("wv", [P, KD, D])
        wo = sb("wo", [P, KD, D])
        bq = sb("bq", [P, KD])
        bk = sb("bk", [P, KD])
        bv_all = sb("bv_all", [P, 2, D])
        bo_all = sb("bo_all", [P, D])
        gates_in = sb("gates_in", [P, 2])
        gates = sb("gates", [P, 2])
        identity = sb("identity", [P, P])
        identity_bf = sb("identity_bf", [P, P], BF16)
        causal_bf = sb("causal_bf", [P, KB], BF16)
        minus_half = sb("minus_half", [P, TT])
        stats = sb("stats", [P, TT, 6])
        mean_var = sb("mean_var", [P, TT, 2])
        var_eps = sb("var_eps", [P, TT])
        rstd = sb("rstd", [P, TT])
        ln_fence = sb("ln_fence", [P, 1])
        x1_bn = sb("x1_bn", [P, TT, 6])
        x1_eps = sb("x1_eps", [P, TT])
        gate_rows = sb("gate_rows", [E, D])
        gateT = sb("gateT", [P, KD, GC])
        expert_rows = split[:].rearrange("p j h t -> p (j h t)").bitcast(F32).rearrange(
            "p (e d) -> p e d", d=D)
        expertT = sb("expertT", [P, KD, E, D])
        first_wins = sb("first_wins", [P, TT, E])
        x1_rows = sb("x1_rows", [P, TT, ROW])
        x1T = sb("x1T", [P, KD, T])
        gated_identity = xhat[:, 0:KD, :]
        gate_mean = sb("gate_mean", [E, 1])
        best = sb("best", [P, TT])
        ranked = sb("ranked", [P, TT, E])
        top_rank = sb("top_rank", [P, TT])
        onehot = sb("onehot", [P, TT, E], BF16)
        batch_seen = sb("batch_seen", [P, E], BF16)
        seen = sb("seen", [P, E], BF16)
        place = sb("place", [P, TT, E])
        dest_f = sb("dest_f", [P, TT])
        dest = sb("dest", [P, TT], U32)
        ids = sb("ids", [P, NT], U32)
        region_base = sb("region_base", [P, TT, E])
        earlier_bf = sb("earlier_bf", [P, P], BF16)
        ones_bf = sb("ones_bf", [P, P], BF16)
        padding = sb("padding", [P, ROW])
        thresholds = sb("thresholds", [1, E, NT])
        upto = sb("upto", [1, E, E])
        tile_no = sb("tile_no", [1, EARLY, E])
        past = sb("past", [1, E, NT])
        tiles_of = sb("tiles_of", [1, E])
        tiles_upto = sb("tiles_upto", [1, E, E])
        ends = sb("ends", [1, E])
        used = sb("used", [1, E + 1])
        drop = sb("drop", [1, E])
        logitsT = sb("logitsT", [P, P])
        ended = x1T[0:1, 0, 0:EARLY * E].rearrange("p (r e) -> p r e", e=E)
        ended_tiles = x1T[0:1, 1, 0:EARLY * E].rearrange("p (r e) -> p r e", e=E)
        expert_f = sb("expert_f", [1, EARLY])
        first_tile = sb("first_tile", [1, EARLY])
        in_region = sb("in_region", [1, EARLY])
        row_f = sb("row_f", [1, EARLY])
        tile_expert = sb("tile_expert", [1, ROUTED], I32)
        tile_row = sb("tile_row", [1, ROUTED], I32)
        pad_row = sb("pad_row", [1, E], I32)

        rows_in = probs[:].rearrange("p r g t -> p (r g t)")[:, 0:SLOTS * ROW].rearrange(
            "p (s r) -> p s r", r=ROW)
        v_flat = v_rows[:].rearrange("p a k g d -> p (a k g d)")
        h_rows = v_flat[:, 0:H_SLOTS * D].rearrange("p (s d) -> p s d", d=D)
        hT = v_flat[:, H_SLOTS * D:(H_SLOTS + HT_SLOTS) * D].rearrange(
            "p (s k t) -> p s k t", s=HT_SLOTS, k=KD)

        scores_ps = es.enter_context(nc.psum_tensor("scores_ps", [P, BANKS, T], F32))
        attn_ps = es.enter_context(nc.psum_tensor("attn_ps", [P, KD, T], F32))
        misc_ps = es.enter_context(nc.psum_tensor("misc_ps", [P, 2, T], F32))

        split_dram = nc.dram_tensor("split_dram", [B, 4, 2, P, T], F32, kind="Internal").ap()
        regions = nc.dram_tensor("regions", [E * REGION + P, ROW], F32, kind="Internal").ap()

        wk_loaded = sem("wk_loaded")
        wq_loaded = sem("wq_loaded")
        wv_loaded = sem("wv_loaded")
        wo_loaded = sem("wo_loaded")
        gates_loaded = sem("gates_loaded")
        experts_in = sem("experts_in")
        x_loaded = sem("x_loaded")
        ctx_loaded = sem("ctx_loaded")
        consts_zeroed = sem("consts_zeroed")
        consts_ready = sem("consts_ready")
        kstack_zeroed = sem("kstack_zeroed")
        v_zeroed = sem("v_zeroed")
        gateT_zeroed = sem("gateT_zeroed")
        gates_ready = sem("gates_ready")
        wq_scaled = sem("wq_scaled")
        wo_scaled = sem("wo_scaled")
        ln_stats = sem("ln_stats")
        ln_mean_var = sem("ln_mean_var")
        ln_var_eps = sem("ln_var_eps")
        ln_rstd = sem("ln_rstd")
        x_centred = sem("x_centred")
        xhat_ready = sem("xhat_ready")
        resid_ready = sem("resid_ready")
        ctxT_filled = [sem(f"ctxT_filled{k}") for k in range(KD)]
        ctxT_copied = [sem(f"ctxT_copied{k}") for k in range(KD)]
        xhatT_filled = [sem(f"xhatT_filled{k}") for k in range(KD)]
        xhatT_copied = [sem(f"xhatT_copied{k}") for k in range(KD)]
        proj_filled = [sem(f"proj_filled_{a}{m}") for a, m in PROJ]
        proj_hi = [sem(f"proj_hi_{a}{m}") for a, m in PROJ]
        proj_lo = [sem(f"proj_lo_{a}{m}") for a, m in PROJ]
        split_stored = [sem(f"split_stored_{a}{m}") for a, m in PROJ]
        stack_loaded = [sem(f"stack_loaded{h}") for h in range(KD)]
        v_filled = [sem(f"v_filled{i}") for i in range(2)]
        v_copied = [sem(f"v_copied{i}") for i in range(2)]
        scores_done = sem("scores_done")
        half_scored = [sem(f"half_scored{h}") for h in range(KD)]
        max_done = sem("max_done")
        exp_done = sem("exp_done")
        zinv_done = sem("zinv_done")
        v_scaled_done = sem("v_scaled_done")
        pv_done = sem("pv_done")
        attn_copied = [sem(f"attn_copied{h}") for h in range(KD)]
        y_filled = [sem(f"y_filled{i}") for i in range(2)]
        y_added = [sem(f"y_added{i}") for i in range(2)]
        expertT_filled = sem("expertT_filled")
        expertT_copied = sem("expertT_copied")
        gateT_filled = sem("gateT_filled")
        gateT_copied = sem("gateT_copied")
        gate_step = sem("gate_step")
        gated_identity_zeroed = sem("gated_identity_zeroed")
        gated_identity_ready = sem("gated_identity_ready")
        shift_ready = sem("shift_ready")
        gate_centred = sem("gate_centred")
        x1T_filled = [sem(f"x1T_filled{k}") for k in range(KD)]
        x1T_copied = [sem(f"x1T_copied{k}") for k in range(KD)]
        x1_stats = sem("x1_stats")
        x1_mean_var = sem("x1_mean_var")
        x1_var_eps = sem("x1_var_eps")
        x1_rstd = sem("x1_rstd")
        logitsT_filled = sem("logitsT_filled")
        logitsT_copied = sem("logitsT_copied")
        logits_filled = sem("logits_filled")
        logits_read = sem("logits_read")
        route = sem("route")
        onehot_ready = sem("onehot_ready")
        rank_filled = sem("rank_filled")
        rank_read = sem("rank_read")
        seen_ready = sem("seen_ready")
        dest_ready = sem("dest_ready")
        regions_stored = sem("regions_stored")
        padding_ready = sem("padding_ready")
        padding_stored = sem("padding_stored")
        counts_filled = sem("counts_filled")
        plan = sem("plan")
        plan_ready = sem("plan_ready")
        last_stored = sem("last_stored")
        tile_loaded = [sem(f"tile_loaded{i}") for i in range(LOADS)]
        h_ready = sem("h_ready")
        hT_filled = sem("hT_filled")
        hT_copied = sem("hT_copied")
        expert_filled = sem("expert_filled")
        expert_read = sem("expert_read")
        row_stored = [sem(f"row_stored{i}") for i in range(SLOTS // GROUP)]

        x_t = x.rearrange("b (t p) d -> b p t d", p=P)
        ctx_t = ctx.rearrange("b (t p) d -> b p t d", p=P)
        out_rows = out.rearrange("b t d -> (b t) d")
        def bank(kind, i, c):
            ahead = isinstance(c, int) and c == 0
            if kind == "ctx":
                return scores_ps[:, i] if ahead else misc_ps[:, i]
            if kind == "proj":
                return scores_ps[:, (2, 3, 0, 1)[i]] if ahead else misc_ps[:, PROJ_BANK[i]]
            if kind == "v":
                return attn_ps[:, i if ahead else 0]
            assert kind == "xhat"
            return misc_ps[:, i]

        y_banks = attn_ps[:, 1], misc_ps[:, 0]
        hT_banks = [scores_ps[:, i, 0:D] for i in range(HT_SLOTS)]
        expert_banks = [scores_ps[:, 3, 0:D], attn_ps[:, 0, 0:D]]

        block = es.enter_context(nc.Block())

        @block.sync
        def _(sp):
            def on_all(v):
                return v.rearrange("(a n) -> a n", a=1).partition_broadcast(P)

            def load_x(c):
                sp.dma_start(x_ring[:, bass.ds(TT * (c % 4), TT), :],
                             x_t[bass.ds(c, 1)].rearrange("a p t d -> (a p) t d")).then_inc(x_loaded, 16)

            def load_ctx(c):
                sp.dma_start(ctx_in[:], ctx_t[bass.ds(c, 1)].rearrange("a p t d -> (a p) t d"))\
                    .then_inc(ctx_loaded, 16)

            def store_split(c, j):
                sp.wait_ge(proj_lo[j], c + 1)
                sp.wait_ge(proj_hi[j], c + 1)
                sp.dma_start(split_dram[bass.ds(c, 1), j].rearrange("a h p t -> (a p) h t"),
                             split[:, j].bitcast(F32)).then_inc(split_stored[j], 16)

            def load_stack(c, h, a, free=None, count=0):
                stack = (kstack, qstack)[a][h]
                sp.wait_ge(split_stored[2 * a + h], 16 * (c + 1))
                if free is not None:
                    sp.wait_ge(free, count)
                for head in range(2):
                    for prod in range(4):
                        part = prod % 2 if a == 0 else prod // 2
                        src = split_dram[bass.ds(c, 1), 2 * a + h, part].rearrange(
                            "a (g s d) t -> s (a d) g t", s=2, d=HD)[head]
                        row = 64 * head + HD * prod
                        dst = stack[row:row + HD, :, head, :] if a == 0 else stack[row:row + HD, :, :]
                        sp.dma_start(dst.bitcast(F32), src).then_inc(stack_loaded[h], 16)

            def load_bias(dst, v, done):
                for k in range(KD):
                    sp.dma_start(dst[:, k:k + 1], v.rearrange("(k p a) -> k p a", p=P, a=1)[k])\
                        .then_inc(done, 16)

            def load_weights(dst, w, done):
                sp.dma_start(dst[:], w.rearrange("(k p) n -> p k n", p=P)).then_inc(done, 16)

            load_ctx(0)
            load_bias(bk, b_k, wk_loaded)
            load_weights(wk, w_k, wk_loaded)
            load_x(0)
            load_bias(bq, b_q, wq_loaded)
            load_weights(wq, w_q, wq_loaded)
            sp.dma_start(gate_rows[:], gate_w).then_inc(experts_in, 16)
            for i, g in enumerate((g_xattn, g_ffn)):
                sp.dma_start(gates_in[:, i:i + 1], on_all(g)).then_inc(gates_loaded, 16)
            load_weights(wv, w_v, wv_loaded)
            for i in range(2):
                sp.dma_start(bv_all[:, i, :], on_all(b_v)).then_inc(wv_loaded, 16)
            for k in range(KD):
                sp.wait_ge(ctxT_filled[k], 1)
            load_ctx(1)
            store_split(0, 0)
            load_weights(wo, w_o, wo_loaded)
            sp.dma_start(bo_all[:], on_all(b_o)).then_inc(wo_loaded, 16)
            load_x(1)
            load_stack(0, 0, 0)
            load_stack(0, 0, 1)
            store_split(0, 1)
            store_split(0, 3)

            def iteration(b, first=False, tokens=True, prep=True):
                if not first:
                    sp.wait_ge(half_scored[1], b)
                if tokens:
                    load_x(b + 2)
                load_stack(b, 1, 0)
                load_stack(b, 1, 1)
                if tokens:
                    for k in range(KD):
                        sp.wait_ge(ctxT_filled[k], b + 2)
                    load_ctx(b + 2)
                if prep:
                    for j in (0, 1, 2):
                        store_split(b + 1, j)
                    load_stack(b + 1, 0, 0, half_scored[0], b + 1)
                    load_stack(b + 1, 0, 1)
                    store_split(b + 1, 3)

            sp.wait_ge(x_loaded, 32)
            iteration(0, first=True)
            with sp.Fori(1, B - 2) as b:
                iteration(b)
            iteration(B - 2, tokens=False)
            for j in range(4):
                sp.wait_ge(split_stored[j], 16 * B)
            sp.dma_start(expert_rows, expert_w.rearrange("e (k p) h -> p (e k) h", p=P))\
                .then_inc(experts_in, 16)
            iteration(B - 1, tokens=False, prep=False)

            def load_tiles(ks):
                _, places = nc.values_load_multi_w_load_instructions(
                    tile_row[0:1, ks[0]:ks[-1] + 1], engines=[mybir.EngineType.SP],
                    min_val=0, max_val=E * REGION)
                if ks[0] >= SLOTS:
                    sp.wait_ge(row_stored[ks[0] % SLOTS // GROUP], 16 * GROUP)
                for k, at in zip(ks, places):
                    if k >= LOADS:
                        sp.wait_ge(tile_loaded[k % LOADS], 16 * (k // LOADS))
                    sp.dma_start(rows_in[:, k % SLOTS, :], regions[bass.ds(at, P), :])\
                        .then_inc(tile_loaded[k % LOADS], 16)

            sp.wait_ge(plan_ready, 1)
            sp.wait_ge(regions_stored, 16 * (NT - TT) + 16)
            sp.wait_ge(pv_done, BLOCKS * B)
            for k in range(0, BEFORE_PAD, GROUP):
                load_tiles(range(k, k + GROUP))
            sp.wait_ge(plan_ready, 2)
            _, ends_at = nc.values_load_multi_w_load_instructions(
                pad_row[0:1, 0:E // 2], engines=[mybir.EngineType.SP], min_val=0,
                max_val=(E - 1) * REGION + B * T)
            for at in ends_at:
                sp.dma_start(regions[bass.ds(at, P), :], padding[:]).then_inc(padding_stored, 16)
            for k in range(BEFORE_PAD, EARLY, GROUP):
                load_tiles(range(k, k + GROUP))
            sp.wait_ge(plan_ready, 3)
            sp.wait_ge(last_stored, 16 * TT)
            sp.wait_ge(padding_stored, 16 * E)
            for k in range(EARLY, ROUTED, GROUP):
                load_tiles(range(k, k + GROUP))
            for i in range(EARLY // GROUP):
                sp.wait_ge(row_stored[i], 16 * GROUP * (2 if GROUP * i < LATE else 1))

        @block.gpsimd
        def _(pool):
            nc.gpsimd.memset(identity[:], 0.0)
            nc.gpsimd.memset(identity_bf[:], 0.0)
            nc.gpsimd.memset(causal_bf[:], 0.0)
            nc.gpsimd.memset(minus_half[:], -0.5).then_inc(consts_zeroed, 1)
            pool.wait_ge(consts_zeroed, 1)
            for m in (identity, identity_bf):
                nc.gpsimd.affine_select(out=m[:], in_=m[:], compare_op=ALU.not_equal, fill=1.0, base=0,
                                        pattern=[[-1, P]], channel_multiplier=1)
            for rows, base, done in ((P, KB, consts_zeroed), (KB, 0, consts_ready)):
                last = nc.gpsimd.affine_select(out=causal_bf[0:rows], in_=causal_bf[0:rows],
                                               compare_op=ALU.is_ge, fill=NEG, base=base,
                                               pattern=[[1, KB]], channel_multiplier=-1)
                last.then_inc(done, 1)
                pool.wait_ge(done, 2 if rows == P else 1)

            nc.gpsimd.iota(ids[:], pattern=[[P, NT]], base=0, channel_multiplier=1)
            for t in range(TT):
                nc.gpsimd.iota(region_base[:, t, :], pattern=[[REGION, E]], base=0, channel_multiplier=0,
                               allow_small_or_imprecise_dtypes=True)
                nc.gpsimd.iota(first_wins[:, t, :], pattern=[[-1, E]], base=E, channel_multiplier=0,
                               allow_small_or_imprecise_dtypes=True)
            nc.gpsimd.iota(thresholds[:], pattern=[[0, E], [P, NT]], base=0, channel_multiplier=0,
                           allow_small_or_imprecise_dtypes=True)
            nc.gpsimd.iota(tile_no[:], pattern=[[1, EARLY], [0, E]], base=0, channel_multiplier=0,
                           allow_small_or_imprecise_dtypes=True)
            nc.gpsimd.memset(padding[:], 0.0)
            nc.gpsimd.memset(upto[:], 1.0)
            nc.gpsimd.memset(earlier_bf[:], 1.0)
            nc.gpsimd.memset(seen[:], 0.0).then_inc(seen_ready, 1)
            nc.gpsimd.memset(ones_bf[:], 1.0).then_inc(consts_zeroed, 1)
            pool.wait_ge(consts_zeroed, 3)
            nc.gpsimd.iota(padding[:, ID:ID + 1].bitcast(U32), pattern=[[0, 1]], base=B * T,
                           channel_multiplier=1).then_inc(padding_ready, 1)
            nc.gpsimd.affine_select(out=upto[:], in_=upto[:], compare_op=ALU.is_ge, fill=0.0, base=0,
                                    pattern=[[1, E], [-1, E]], channel_multiplier=0)
            nc.gpsimd.affine_select(out=earlier_bf[:], in_=earlier_bf[:], compare_op=ALU.is_gt, fill=0.0,
                                    base=0, pattern=[[1, P]], channel_multiplier=-1)\
                .then_inc(consts_ready, 1)

            def rstd_of(c):
                pool.wait_ge(ln_var_eps, c + 1)
                nc.gpsimd.tensor_tensor(rstd[:], var_eps[:], minus_half[:], ALU.pow).then_inc(ln_rstd, 1)

            def x_row(c, t):
                return x_ring[:, bass.ds(TT * (c % 4) + t, 1), :].rearrange("p a d -> p (a d)")

            def centre(c, ts):
                if 0 in ts:
                    for k in range(KD):
                        pool.wait_ge(xhatT_filled[k], c)
                for t in ts:
                    last = nc.gpsimd.tensor_tensor(xhat[:, t, :], x_row(c, t),
                                                   mean_var[:, t, 0:1].to_broadcast([P, D]), ALU.subtract)
                if TT - 1 in ts:
                    last.then_inc(x_centred, 1)

            def normalise_x(c, ts):
                if 0 in ts:
                    pool.wait_ge(x_centred, c)
                    pool.wait_ge(ln_rstd, c + 1)
                for t in ts:
                    last = nc.gpsimd.tensor_tensor(xhat[:, t, :], xhat[:, t, :],
                                                   rstd[:, t:t + 1].to_broadcast([P, D]), ALU.mult)
                if TT - 1 in ts:
                    last.then_inc(xhat_ready, 1)

            def residual(c, ts):
                if 0 in ts:
                    pool.wait_ge(wo_scaled, 1)
                    pool.wait_ge(xhat_ready, c + 1)
                for t in ts:
                    last = nc.gpsimd.tensor_tensor(x_row(c, t), x_row(c, t), bo_all[:], ALU.add)
                if TT - 1 in ts:
                    last.then_inc(resid_ready, 1)

            def x1_rstd_of(c):
                pool.wait_ge(x1_var_eps, c + 1)
                nc.gpsimd.tensor_tensor(x1_rows[:, :, RSTD], x1_eps[:], minus_half[:], ALU.pow)\
                    .then_inc(x1_rstd, 1)

            def scatter(c, t):
                if t == 0:
                    pool.wait_ge(padding_ready, 1)
                    pool.wait_ge(dest_ready, c + 1)
                    pool.wait_ge(x1_rstd, c + 1)
                    pool.wait_ge(shift_ready, c + 1)
                nc.gpsimd.indirect_dma_start(
                    regions[:, :], bass.IndirectOffsetOnAxis(ap=dest[:, t:t + 1], axis=0),
                    x1_rows[:, t, :], None)\
                    .then_inc(last_stored if isinstance(c, int) and c == B - 1 else regions_stored, 16)

            def scale_v(b, blk):
                if blk < 0:
                    b, blk = b - 1, blk + BLOCKS
                pool.wait_ge(zinv_done, BLOCKS * b + blk + 1)
                if not (isinstance(b, int) and BLOCKS * b + blk < RING):
                    pool.wait_ge(pv_done, BLOCKS * b + blk - RING + 1)
                if blk == 0:
                    pool.wait_ge(v_copied[0], b + 1)
                    pool.wait_ge(v_copied[1], b + 1)
                h, kb = blk // NKB, KEY_BLOCKS[blk % NKB]
                slot = blk % RING
                rows = v_rows[:, bass.ds(b % 2, 1), kb, PAIRS * h:PAIRS * (h + 1), :]
                rows = rows.rearrange("p a g d -> p (a g) d")
                nc.gpsimd.tensor_tensor(v_scaled[:, slot], rows,
                                        z_inv[:, slot, :].unsqueeze(2).to_broadcast([P, PAIRS, 2 * HD]),
                                        ALU.mult).then_inc(v_scaled_done, 1)

            def iteration(b, first=False, ln=True):
                for blk in range(BLOCKS):
                    if not (first and blk < 2):
                        scale_v(b, blk - 2)
                    for i in range(2):
                        two = range(2 * i, 2 * i + 2)
                        if blk == AT_RESIDUAL[i] and not first:
                            residual(b, two)
                        if ln and blk == AT_CENTRE[i]:
                            centre(b + 2, two)
                        if ln and blk == AT_NORMALISE[i]:
                            normalise_x(b + 2, two)
                        if blk == AT_SCATTER[i] and not first:
                            for t in two:
                                scatter(b - 1, t)
                    if blk == AT_X1_RSTD and not first:
                        x1_rstd_of(b - 1)
                    if blk in (12, 13) and first:
                        residual(0, range(2 * (blk - 12), 2 * (blk - 11)))
                    if ln and blk == AT_RSTD:
                        rstd_of(b + 2)

            rstd_of(0)
            for i in range(2):
                nc.gpsimd.memset(v_rows[:, i], 0.0).then_inc(v_zeroed, 1)
            rstd_of(1)
            centre(1, range(TT))
            normalise_x(1, range(TT))
            pool.wait_ge(padding_ready, 1)
            pool.dma_start(regions[E * REGION:E * REGION + P, :], padding[:]).then_inc(regions_stored, 16)
            iteration(0, first=True)
            with pool.Fori(1, B - 2) as b:
                iteration(b)
            iteration(B - 2, ln=False)
            iteration(B - 1, ln=False)
            scale_v(B, -2)
            scale_v(B, -1)

            def store_tile(k):
                pool.wait_ge(expert_read, k + 1)
                s = k % SLOTS
                nc.gpsimd.indirect_dma_start(
                    out_rows, bass.IndirectOffsetOnAxis(ap=rows_in[:, s, ID:ID + 1].bitcast(U32), axis=0),
                    rows_in[:, s, 0:D], None, bounds_check=last_id, oob_is_err=False)\
                    .then_inc(row_stored[s // GROUP], 16)

            last_id = nc.gpsimd.to_reg(B * T - 1)
            for what in ENDING:
                if what == "x1T":
                    x1_rstd_of(B - 1)
                if what == "ranks":
                    for t in range(TT):
                        scatter(B - 1, t)
                if isinstance(what, int):
                    store_tile(what)

        @block.tensor
        def _(pe):
            def transposes(bank, source, k):
                for t in range(TT):
                    last = nc.tensor.transpose(bank[:, P * t:P * (t + 1)],
                                               source[:, t, P * k:P * (k + 1)], identity[:])
                return last

            def transpose_ctx(c, k):
                if k == 0:
                    pe.wait_ge(ctx_loaded, 16 * (c + 1))
                    if not (isinstance(c, int) and c < 2):
                        pe.wait_ge(seen_ready, c - 1)
                    elif c == 1:
                        for i in range(KD):
                            pe.wait_ge(xhatT_copied[i], c)
                transposes(bank("ctx", k, c), ctx_in, k).then_inc(ctxT_filled[k], 1)

            def transpose_xhat(c, k):
                pe.wait_ge(xhat_ready, c + 1)
                if k == 0 and not (isinstance(c, int) and c < 2):
                    pe.wait_ge(y_added[1], c - 1)
                elif not (isinstance(c, int) and c == 0):
                    pe.wait_ge(proj_lo[k], c + 1)
                transposes(bank("xhat", k, c), xhat, k).then_inc(xhatT_filled[k], 1)

            def project(c, j, k):
                a, m = PROJ[j]
                src, w = (ctxT, wk) if a == "k" else (xhatT, wq)
                if k == 0:
                    for i in range(KD):
                        pe.wait_ge(ctxT_copied[i] if a == "k" else xhatT_copied[i], c + 1)
                    if j == 3 and not (isinstance(c, int) and c == 0):
                        pe.wait_ge(proj_lo[2], c + 1)
                half = nc.tensor.matmul(bank("proj", j, c), w[:, k, P * m:P * (m + 1)], src[:, k, :],
                                        start=(k == 0), stop=(k == KD - 1))
                if k == KD - 1:
                    half.then_inc(proj_filled[j], 1)

            def project_v(c, i, t):
                if t == 0:
                    if not (isinstance(c, int) and c == 0):
                        pe.wait_ge(*((v_copied[0], c + 1) if i else (attn_copied[0], c)))
                cols = slice(P * (2 * i + t), P * (2 * i + t + 1))
                for k in range(KD):
                    last = nc.tensor.matmul(bank("v", i, c)[:, D * t:D * (t + 1)], ctxT[:, k, cols],
                                            wv[:, k, :], start=(k == 0), stop=(k == KD - 1))
                if t == 1:
                    last.then_inc(v_filled[i], 1)

            def project_out(c, i, t, bank_free=None, count=0):
                if t == 0:
                    if i == 0:
                        for h in range(KD):
                            pe.wait_ge(attn_copied[h], c + 1)
                    else:
                        pe.wait_ge(bank_free, count)
                cols = slice(P * (2 * i + t), P * (2 * i + t + 1))
                for h in range(KD):
                    last = nc.tensor.matmul(y_banks[i][:, D * t:D * (t + 1)], attnT[:, h, cols],
                                            wo[:, h, :], start=(h == 0), stop=(h == KD - 1))
                if t == 1:
                    last.then_inc(y_filled[i], 1)

            def keys_of(h, g, kb):
                return kstack[h][:, g].rearrange("p s (i kb) -> p (s i) kb", kb=NKB)[:, :, kb]

            def transpose_x1(c, k, bank_free=None, count=0):
                for i in range(2):
                    pe.wait_ge(y_added[i], c + 1)
                if k == 1 and bank_free is not None:
                    pe.wait_ge(bank_free, count)
                transposes((attn_ps[:, 1], misc_ps[:, 1])[k], x1_rows, k).then_inc(x1T_filled[k], 1)

            def gate(c):
                for k in range(KD):
                    pe.wait_ge(x1T_copied[k], c + 1)
                for k in range(KD):
                    for t in range(TT):
                        last = nc.tensor.matmul(attn_ps[GC * t:GC * (t + 1), 1, 0:P], gateT[:, k, :],
                                                x1T[:, k, P * t:P * (t + 1)],
                                                start=(k == 0), stop=(k == KD - 1))
                last.then_inc(logitsT_filled, 1)

            def logits(c):
                pe.wait_ge(logitsT_copied, c + 1)
                last = nc.tensor.transpose(misc_ps[:, 1, 0:P], logitsT[:], identity[:])
                last.then_inc(logits_filled, 1)

            def ranks(c, bank_free, count):
                pe.wait_ge(bank_free, count)
                pe.wait_ge(onehot_ready, c + 1)
                pe.wait_ge(seen_ready, c + 1)
                out_all = misc_ps[:, 0, 0:TT * E]
                nc.tensor.matmul(out_all, earlier_bf[:], onehot[:].rearrange("p t e -> p (t e)"),
                                 start=True, stop=False)
                nc.tensor.matmul(out_all.rearrange("p (t e) -> p t e", t=TT), ones_bf[:],
                                 seen[:].unsqueeze(1).to_broadcast([P, TT, E]), start=False, stop=False)
                for t in range(TT - 1):
                    after = TT - 1 - t
                    last = nc.tensor.matmul(
                        misc_ps[:, 0, E * (t + 1):E * TT].rearrange("p (t e) -> p t e", t=after),
                        ones_bf[:], onehot[:, t:t + 1, :].to_broadcast([P, after, E]),
                        start=False, stop=(t == TT - 2))
                last.then_inc(rank_filled, 1)

            def count_rows(where, batches):
                pe.wait_ge(seen_ready, batches + 1)
                nc.tensor.matmul(where, ones_bf[:], seen[:], start=True, stop=True)\
                    .then_inc(counts_filled, 1)

            def transpose_expert(e):
                for k in range(KD):
                    for f in range(KD):
                        last = nc.tensor.transpose(
                            misc_ps[:, EXPERT_BANK[e], D * k + P * f:D * k + P * (f + 1)],
                            expert_rows[:, KD * e + f, P * k:P * (k + 1)], identity[:])
                last.then_inc(expertT_filled, 1)

            def score(b, n, first):
                blk, g = divmod(n, PAIRS)
                h, kb = blk // NKB, KEY_BLOCKS[blk % NKB]
                L = queries(kb)
                if kb == 0 and g == 0:
                    pe.wait_ge(stack_loaded[h], 16 * STACK_DMAS * (b + 1))
                tiles = range(n, n + AT_ONCE)
                for m in tiles:
                    if not (first and READ_BEFORE[m] < 0):
                        pe.wait_ge(exp_done, TILES * b + READ_BEFORE[m] + 1)
                    product = nc.tensor.matmul(score_columns(m, L), keys_of(h, m % PAIRS, kb),
                                               qstack[h][:, m % PAIRS, KB * kb:T],
                                               start=not (SHORT[blk] and m % 2), stop=False)
                if m % (NKB * PAIRS) == NKB * PAIRS - 1:
                    product.then_inc(half_scored[h], 1)
                if SHORT[blk]:
                    for m in tiles[::2]:
                        both = scores_ps[:, BANK_OF[m], :].rearrange("p (a q) -> p a q", a=2)[:, :, 0:KB]
                        nc.tensor.matmul(both, identity_bf[:],
                                         causal_bf[:].unsqueeze(1).to_broadcast([P, 2, KB]),
                                         start=False, stop=True).then_inc(scores_done, 2)
                else:
                    for m in tiles:
                        nc.tensor.matmul(score_columns(m, KB), identity_bf[:], causal_bf[:],
                                         start=False, stop=True).then_inc(scores_done, 1)

            def times_v(b, blk, first=False):
                if blk < 0:
                    b, blk = b - 1, blk + BLOCKS
                h, kb = blk // NKB, KEY_BLOCKS[blk % NKB]
                if kb == 0:
                    if h == 0:
                        pe.wait_ge(v_copied[1], b + 1)
                    elif not first:
                        pe.wait_ge(logitsT_copied, b)
                    if first and h == 0:
                        pe.wait_ge(v_copied[0], 1)
                pe.wait_ge(v_scaled_done, BLOCKS * b + blk + 1)
                slot = blk % RING
                for g in range(PAIRS):
                    last = nc.tensor.matmul(attn_ps[32 * g:32 * (g + 1), h, KB * kb:T],
                                            v_scaled[:, slot, g, :], probs[:, slot, g, 0:queries(kb)],
                                            start=(kb == 0), stop=(kb == KEY_BLOCKS[-1]))
                last.then_inc(pv_done, 1)

            def prepare(c, n):
                for k in range(KD):
                    if n == AT_CTX[k]:
                        transpose_ctx(c, k)
                    if n == AT_XHAT[k]:
                        transpose_xhat(c, k)
                    for j in range(4):
                        if n == AT_PROJ[j][k]:
                            project(c, j, k)
                for i in range(2):
                    for t in range(2):
                        if n == AT_V[i][t]:
                            project_v(c, i, t)

            def finish(c, n, prep=True):
                for i in range(2):
                    for t in range(2):
                        if n == AT_Y[i][t]:
                            if prep:
                                project_out(c, i, t, proj_lo[0], c + 3)
                            else:
                                project_out(c, i, t, seen_ready, c)
                if n == AT_X1T[0]:
                    transpose_x1(c, 0)
                if n == AT_X1T[1]:
                    if prep:
                        transpose_x1(c, 1, xhatT_copied[1], c + 3)
                    else:
                        transpose_x1(c, 1, expertT_copied, 1)
                if n == AT_GATE:
                    gate(c)
                if n == AT_LOGITS:
                    logits(c)
                if n == AT_RANK:
                    if prep:
                        ranks(c, proj_lo[3], c + 3)
                    else:
                        ranks(c, expertT_copied, 5)

            def iteration(b, first=False, prep=True):
                for n in range(TILES):
                    if n % AT_ONCE == 0:
                        score(b, n, first)
                    if n % PAIRS == AT_PV and not (first and n < LAG * PAIRS):
                        times_v(b, n // PAIRS - LAG, first)
                    if not first:
                        finish(b - 1, n, prep)
                    if prep:
                        prepare(b + 1, n)
                    elif n in AT_EXPERT:
                        e = AT_EXPERT.index(n)
                        if e == 0:
                            pe.wait_ge(experts_in, 32)
                            pe.wait_ge(xhatT_copied[1], B)
                        elif e == 1:
                            pe.wait_ge(y_added[1], B - 1)
                        elif e == 5:
                            pe.wait_ge(logits_read, B - 1)
                        else:
                            pe.wait_ge(expertT_copied, e)
                        transpose_expert(e)
                    if not prep and n == AT_COUNT:
                        count_rows(misc_ps[:, 0, 0:E], b)

            pe.wait_ge(consts_ready, 1)
            transpose_ctx(0, 0)
            transpose_ctx(0, 1)
            pe.wait_ge(wk_loaded, 48)
            for j in (0, 1):
                for k in range(KD):
                    project(0, j, k)
            transpose_xhat(0, 0)
            transpose_xhat(0, 1)
            pe.wait_ge(wq_scaled, 2)
            for j in (2, 3):
                for k in range(KD):
                    project(0, j, k)
            pe.wait_ge(gate_centred, 1)
            for k in range(KD):
                last = nc.tensor.transpose(attn_ps[:, 0, E * k:E * (k + 1)],
                                           gate_rows[:, P * k:P * (k + 1)], identity[0:E, 0:E])
            last.then_inc(gateT_filled, 1)
            pe.wait_ge(wv_loaded, 48)
            pe.wait_ge(gateT_copied, 1)
            for i in range(2):
                for t in range(2):
                    project_v(0, i, t)
            pe.wait_ge(kstack_zeroed, 2)
            for j in range(4):
                pe.wait_ge(proj_lo[j], 1)
            pe.wait_ge(consts_ready, 2)
            iteration(0, first=True)
            with pe.Fori(1, B - 1) as b:
                iteration(b)
            iteration(B - 1, prep=False)
            for blk in range(-LAG, 0):
                times_v(B, blk)

            def transpose_h(k):
                pe.wait_ge(h_ready, k + 1)
                for half in range(KD):
                    last = nc.tensor.transpose(hT_banks[k % HT_SLOTS][:, P * half:P * (half + 1)],
                                               h_rows[:, k % H_SLOTS, P * half:P * (half + 1)],
                                               identity[:])
                last.then_inc(hT_filled, 1)

            def times_expert(k):
                if k in (0, EARLY):
                    pe.wait_ge(plan_ready, 1 if k == 0 else 3)
                e = pe.value_load(tile_expert[0:1, k:k + 1], min_val=0, max_val=E - 1)
                pe.wait_ge(hT_copied, k + 1)
                if k >= 2:
                    pe.wait_ge(expert_read, k - 1)
                for half in range(KD):
                    last = nc.tensor.matmul(expert_banks[k % 2], hT[:, k % HT_SLOTS, half, :],
                                            expertT[:, half, bass.ds(e, 1), :].rearrange(
                                                "p a f -> p (a f)"),
                                            start=(half == 0), stop=(half == KD - 1))
                last.then_inc(expert_filled, 1)

            for what in ENDING:
                if what == "out":
                    for i in range(2):
                        for t in range(2):
                            project_out(B - 1, i, t, plan, 1)
                if what == "x1T":
                    transpose_x1(B - 1, 0)
                    transpose_x1(B - 1, 1, expertT_copied, E)
                    transpose_h(0)
                    transpose_h(1)
                if what == "gate":
                    gate(B - 1)
                if what == "logits":
                    logits(B - 1)
                if what == "ranks":
                    ranks(B - 1, y_added[1], B)
                if what == "counts":
                    count_rows(attn_ps[:, 1, 0:E], B)
                if isinstance(what, int):
                    if what + 2 < ROUTED:
                        transpose_h(what + 2)
                    times_expert(what)

        @block.scalar
        def _(act):
            def copy(dst, src, filled, count, copied):
                act.wait_ge(filled, count)
                nc.scalar.copy(dst, src).then_inc(copied, 1)

            def split_hi(c, j):
                a, m = PROJ[j]
                act.wait_ge(proj_filled[j], c + 1)
                if not (isinstance(c, int) and c == 0):
                    act.wait_ge(split_stored[j], 16 * c)
                nc.scalar.activation(split_order(split[:, j, 0, :], j), natural(bank("proj", j, c)),
                                     ACT.Identity,
                                     bias=(bk if a == "k" else bq)[:, m:m + 1]).then_inc(proj_hi[j], 1)

            def copy_attn(b, h):
                act.wait_ge(pv_done, BLOCKS * b + NKB * (h + 1))
                nc.scalar.copy(attnT[:, h, :], attn_ps[:, h, :]).then_inc(attn_copied[h], 1)

            def exps(b, n, first):
                blk, g = divmod(n, PAIRS)
                slot = blk % RING
                act.wait_ge(max_done, TILES * b + n + 1)
                if g == 0 and not (first and blk < RING):
                    act.wait_ge(pv_done, BLOCKS * b + blk - RING + 1)
                L = queries(KEY_BLOCKS[blk % NKB])
                nc.scalar.activation(probs[:, slot, g, 0:L], score_columns(n, L), ACT.Exp,
                                     bias=neg_max[:, slot, g:g + 1],
                                     accum_out=z_sum[:, slot, g:g + 1]).then_inc(exp_done, 1)

            def prepare(c, n):
                if n == AT_CTX[0]:
                    if not (isinstance(c, int) and c == 0):
                        act.wait_ge(v_filled[1], c)
                    copy(ctxT[:, 0, :], bank("ctx", 0, c), ctxT_filled[0], c + 1, ctxT_copied[0])
                if n == AT_XHAT[0]:
                    if not (isinstance(c, int) and c == 0):
                        act.wait_ge(proj_filled[3], c)
                    copy(xhatT[:, 0, :], misc_ps[:, 0, :], xhatT_filled[0], c + 1, xhatT_copied[0])
                for j in range(4):
                    if n == AT_PROJ[j][1]:
                        split_hi(c, j)

            def copy_x1T(c, k):
                copy(x1T[:, k, :], (attn_ps[:, 1, :], misc_ps[:, 1, :])[k], x1T_filled[k], c + 1,
                     x1T_copied[k])

            def copy_logits(c):
                copy(logitsT[:], attn_ps[:, 1, 0:P], logitsT_filled, c + 1, logitsT_copied)

            def iteration(b, first=False, last=False):
                for n in range(TILES):
                    if not last:
                        prepare(b + 1, n)
                    if n == AT_ATTN[1] and not first:
                        copy_attn(b - 1, 1)
                    if n in AT_X1T and not first:
                        copy_x1T(b - 1, AT_X1T.index(n))
                    if n == AT_GATE and not first:
                        copy_logits(b - 1)
                    if n == AT_ATTN[0]:
                        copy_attn(b, 0)
                    exps(b, n, first)

            prepare(0, AT_CTX[0])
            act.wait_ge(wq_loaded, 48)
            nc.scalar.mul(wq[:], wq[:], SCALE).then_inc(wq_scaled, 1)
            nc.scalar.mul(bq[:], bq[:], SCALE).then_inc(wq_scaled, 1)
            act.wait_ge(wk_loaded, 48)
            prepare(0, AT_PROJ[0][1])
            prepare(0, AT_PROJ[1][1])
            act.wait_ge(wq_scaled, 2)
            for n in (AT_XHAT[0], AT_PROJ[2][1], AT_PROJ[3][1]):
                prepare(0, n)
            act.wait_ge(proj_lo[2], 1)
            act.dma_start(split_dram[0, 2].rearrange("h p t -> p h t"), split[:, 2].bitcast(F32))\
                .then_inc(split_stored[2], 16)
            act.wait_ge(gates_loaded, 32)
            nc.scalar.activation(gates[:], gates_in[:], ACT.Tanh).then_inc(gates_ready, 1)
            act.wait_ge(gateT_filled, 1)
            nc.scalar.copy(gateT[:, :, 0:E], attn_ps[:, 0, 0:KD * E].rearrange("p (k e) -> p k e", k=KD))\
                .then_inc(gateT_copied, 1)
            iteration(0, first=True)
            with act.Fori(1, B - 1) as b:
                iteration(b)
            iteration(B - 1, last=True)
            copy_attn(B - 1, 1)

            def pad(e):
                at = act.value_load(pad_row[0:1, e:e + 1], min_val=0, max_val=(E - 1) * REGION + B * T)
                act.dma_start(regions[bass.ds(at, P), :], padding[:]).then_inc(padding_stored, 16)

            def normalise(k):
                act.wait_ge(tile_loaded[k % LOADS], 16 * (k // LOADS + 1))
                row = rows_in[:, k % SLOTS, :]
                nc.scalar.activation(h_rows[:, k % H_SLOTS, :], row[:, 0:D], ACT.Identity,
                                     bias=row[:, SHIFT:SHIFT + 1],
                                     scale=row[:, RSTD:RSTD + 1]).then_inc(h_ready, 1)

            for what in ENDING:
                if what == "out":
                    for k in range(4):
                        normalise(k)
                if what == "x1T":
                    for k in range(KD):
                        copy_x1T(B - 1, k)
                if what == "gate":
                    copy_logits(B - 1)
                if isinstance(what, int):
                    copy(hT[:, what % HT_SLOTS].rearrange("p k t -> p (k t)"),
                         hT_banks[what % HT_SLOTS], hT_filled, what + 1, hT_copied)
                    if what + 4 < ROUTED:
                        normalise(what + 4)
                    if what in AT_PAD:
                        if what == AT_PAD[0]:
                            act.wait_ge(plan_ready, 2)
                        pad(E // 2 + AT_PAD.index(what))

        @block.vector
        def _(dve):
            def zero_stack(h):
                nc.vector.memset(kstack[h][0:64, :, 1, :].bitcast(F32), 0.0)
                nc.vector.memset(kstack[h][64:128, :, 0, :].bitcast(F32), 0.0).then_inc(kstack_zeroed, 1)

            def centre_gate():
                dve.wait_ge(experts_in, 16)
                nc.vector.memset(gateT[:, :, E:], 0.0).then_inc(gateT_zeroed, 1)
                nc.vector.reduce_sum(gate_mean[:], gate_rows[:], AX_X).then_inc(gate_step, 1)
                dve.wait_ge(gate_step, 1)
                nc.vector.tensor_scalar(gate_mean[:], gate_mean[:], 1.0 / D, None, ALU.mult)\
                    .then_inc(gate_step, 1)
                dve.wait_ge(gate_step, 2)
                nc.vector.tensor_scalar(gate_rows[:], gate_rows[:], gate_mean[:], None, ALU.subtract)\
                    .then_inc(gate_centred, 1)

            def scale_wo():
                dve.wait_ge(gates_ready, 1)
                dve.wait_ge(wo_loaded, 32)
                nc.vector.tensor_scalar(wo[:], wo[:], gates[:, 0:1], None, ALU.mult)
                nc.vector.tensor_scalar(bo_all[:], bo_all[:], gates[:, 0:1], None, ALU.mult)\
                    .then_inc(wo_scaled, 1)

            def split_lo(c, j):
                a, m = PROJ[j]
                dve.wait_ge(proj_hi[j], c + 1)
                nc.vector.scalar_tensor_tensor(
                    split_order(split[:, j, 1, :], j), natural(bank("proj", j, c)),
                    (bk if a == "k" else bq)[:, m:m + 1],
                    split_order(split[:, j, 0, :], j).bitcast(F32), ALU.add, ALU.subtract).then_inc(proj_lo[j], 1)

            def copy_v(c, i, s):
                if s == 0:
                    dve.wait_ge(v_filled[i], c + 1)
                for head in range(2):
                    dst = v_rows[64 * head:64 * (head + 1), bass.ds(c % 2, 1),
                                 4 * i + s:4 * i + s + 3:2, :, HD * head:HD * (head + 1)]
                    src = bank("v", i, c)[64 * s:64 * (s + 1)].rearrange(
                        "p (t g s d) -> p s t g d", t=2, s=2, d=HD)[:, head]
                    bias = bv_all[64 * s:64 * (s + 1)].rearrange(
                        "p t (g s d) -> p s t g d", s=2, d=HD)[:, head]
                    last = nc.vector.tensor_tensor(dst.rearrange("p a t g d -> p (a t) g d"), src,
                                                   bias, ALU.add)
                if s == 1:
                    last.then_inc(v_copied[i], 1)

            def add_y(b, i):
                dve.wait_ge(y_filled[i], b + 1)
                if i == 0:
                    dve.wait_ge(resid_ready, b + 1)
                    dve.wait_ge(regions_stored, 16 * TT * b + 16)
                nc.vector.tensor_tensor(x1_rows[:, 2 * i:2 * i + 2, 0:D],
                                        y_banks[i].rearrange("p (t d) -> p t d", t=2),
                                        x_ring[:, bass.ds(TT * (b % 4) + 2 * i, 2), :], ALU.add)\
                    .then_inc(y_added[i], 1)

            def after(c, k):
                dve.wait_ge(route, ROUTE_STEPS * c + k)

            def finish(c, n):
                for i in range(2):
                    if n == AT_Y[i][1]:
                        add_y(c, i)
                if n in AT_X1_STATS:
                    t = AT_X1_STATS.index(n)
                    if t == 0:
                        dve.wait_ge(y_added[0], c + 1)
                        dve.wait_ge(y_added[1], c + 1)
                        nc.vector.tensor_copy(x1_rows[:, :, ID].bitcast(U32),
                                              ids[:, bass.ds(TT * c, TT)])
                    last = nc.vector.bn_stats(x1_bn[:, t, :], x1_rows[:, t, 0:D])
                    if t == TT - 1:
                        last.then_inc(x1_stats, 1)
                logits = misc_ps[:, 1, 0:P].rearrange("p (t e) -> p t e", t=TT)[:, :, 0:E]
                rank = misc_ps[:, 0, 0:TT * E].rearrange("p (t e) -> p t e", t=TT)

                def over_experts(v):
                    return v.unsqueeze(2).to_broadcast([P, TT, E])

                if n == AT_X1_VAR[0]:
                    dve.wait_ge(x1_stats, c + 1)
                    nc.vector.memset(ln_fence[:], 0.0)
                    for t in range(TT):
                        last = nc.vector.bn_aggr(x1_rows[:, t, MEAN:VAR + 1], x1_bn[:, t, :])
                    last.then_inc(x1_mean_var, 1)
                if n == AT_X1_VAR[1]:
                    dve.wait_ge(x1_mean_var, c + 1)
                    nc.vector.tensor_scalar(x1_eps[:], x1_rows[:, :, VAR], EPS, None, ALU.add)\
                        .then_inc(x1_var_eps, 1)
                if n == AT_LOGITS:
                    dve.wait_ge(logits_filled, c + 1)
                    nc.vector.reduce_max(best[:], logits, AX_X).then_inc(route, 1)
                if n == AT_LOGITS + 1:
                    after(c, 1)
                    nc.vector.tensor_tensor(ranked[:], logits, over_experts(best[:]), ALU.is_equal)\
                        .then_inc(logits_read, 1)
                    dve.wait_ge(logits_read, c + 1)
                    nc.vector.tensor_tensor(ranked[:], ranked[:], first_wins[:], ALU.mult)\
                        .then_inc(route, 1)
                if n == AT_LOGITS + 2:
                    after(c, 2)
                    nc.vector.reduce_max(top_rank[:], ranked[:], AX_X).then_inc(route, 1)
                if n == AT_LOGITS + 3:
                    after(c, 3)
                    nc.vector.tensor_tensor(onehot[:], ranked[:], over_experts(top_rank[:]), ALU.is_equal)\
                        .then_inc(onehot_ready, 1)
                if n == AT_RANK - 1:
                    dve.wait_ge(x1_rstd, c + 1)
                    nc.vector.scalar_tensor_tensor(x1_rows[:, :, SHIFT], x1_rows[:, :, MEAN], -1.0,
                                                   x1_rows[:, :, RSTD], ALU.mult, ALU.mult)\
                        .then_inc(shift_ready, 1)
                if n == AT_RANK:
                    dve.wait_ge(rank_filled, c + 1)
                    nc.vector.tensor_tensor(place[:], rank, region_base[:], ALU.add)\
                        .then_inc(rank_read, 1)
                    with nc.allow_low_precision(reason="counts up to NT, exact in bfloat16"):
                        nc.vector.reduce_sum(batch_seen[:], onehot[:].rearrange("p t e -> p e t"), AX_X)\
                            .then_inc(route, 1)
                if n == AT_RANK + 1:
                    dve.wait_ge(rank_read, c + 1)
                    nc.vector.tensor_tensor(place[:], place[:], onehot[:], ALU.mult).then_inc(route, 1)
                if n == AT_RANK + 2:
                    after(c, 5)
                    nc.vector.reduce_sum(dest_f[:], place[:], AX_X).then_inc(route, 1)
                    nc.vector.tensor_tensor(seen[:], seen[:], batch_seen[:], ALU.add)\
                        .then_inc(seen_ready, 1)
                if n == AT_RANK + 3:
                    after(c, 6)
                    nc.vector.tensor_copy(dest[:], dest_f[:]).then_inc(dest_ready, 1)

            def maxes(b, n):
                blk, g = divmod(n, PAIRS)
                L = queries(KEY_BLOCKS[blk % NKB])
                if not SHORT[blk]:
                    dve.wait_ge(scores_done, TILES * b + n + 1)
                    nc.vector.tensor_reduce(neg_max[:, blk % RING, g:g + 1], score_columns(n, L),
                                            AX_X, ALU.max, negate=True).then_inc(max_done, 1)
                elif n % 2 == 0:
                    dve.wait_ge(scores_done, TILES * b + n + 2)
                    both = scores_ps[:, BANK_OF[n], :].rearrange("p (a q) -> p a q", a=2)[:, :, 0:L]
                    nc.vector.tensor_reduce(neg_max[:, blk % RING, g:g + 2], both,
                                            AX_X, ALU.max, negate=True).then_inc(max_done, 2)

            def invert_z(b, blk):
                if blk < 0:
                    b, blk = b - 1, blk + BLOCKS
                dve.wait_ge(exp_done, TILES * b + PAIRS * (blk + 1))
                nc.vector.reciprocal(z_inv[:, blk % RING, :], z_sum[:, blk % RING, :])\
                    .then_inc(zinv_done, 1)

            def layernorm(c, n):
                if n in AT_X_STATS:
                    t = AT_X_STATS.index(n)
                    if t == 0:
                        dve.wait_ge(x_loaded, 16 * (c + 1))
                    row = x_ring[:, bass.ds(TT * (c % 4) + t, 1), :].rearrange("p a d -> p (a d)")
                    last = nc.vector.bn_stats(stats[:, t, :], row)
                    if t == TT - 1:
                        last.then_inc(ln_stats, 1)
                if n == AT_X_VAR[0]:
                    dve.wait_ge(ln_stats, c + 1)
                    if not (isinstance(c, int) and c == 0):
                        dve.wait_ge(xhat_ready, c)
                    nc.vector.memset(ln_fence[:], 0.0)
                    for t in range(TT):
                        last = nc.vector.bn_aggr(mean_var[:, t, :], stats[:, t, :])
                    last.then_inc(ln_mean_var, 1)
                if n == AT_X_VAR[1]:
                    dve.wait_ge(ln_mean_var, c + 1)
                    nc.vector.tensor_scalar(var_eps[:], mean_var[:, :, 1], EPS, None, ALU.add)\
                        .then_inc(ln_var_eps, 1)

            def normalise_first():
                dve.wait_ge(ln_rstd, 1)
                for t in range(TT):
                    last = nc.vector.tensor_scalar(xhat[:, t, :], x_ring[:, t, :], mean_var[:, t, 0:1],
                                                   rstd[:, t:t + 1], ALU.subtract, ALU.mult)
                last.then_inc(xhat_ready, 1)

            def prepare(c, n):
                if n == AT_CTX[1]:
                    if not (isinstance(c, int) and c == 0):
                        dve.wait_ge(v_filled[1], c)
                    dve.wait_ge(ctxT_filled[1], c + 1)
                    nc.vector.tensor_copy(ctxT[:, 1, :], bank("ctx", 1, c)).then_inc(ctxT_copied[1], 1)
                if n == AT_XHAT[1]:
                    dve.wait_ge(xhatT_filled[1], c + 1)
                    if not (isinstance(c, int) and c == 0):
                        dve.wait_ge(proj_filled[3], c)
                    nc.vector.tensor_copy(xhatT[:, 1, :], misc_ps[:, 1, :]).then_inc(xhatT_copied[1], 1)
                for j in range(4):
                    if n == AT_PROJ[j][1] + LO_LATER:
                        split_lo(c, j)
                for i in range(2):
                    for s in range(2):
                        if n == AT_V[i][1] + s:
                            copy_v(c, i, s)

            def gate_identity(n):
                if n == AT_IDENTITY[0]:
                    for k in range(KD):
                        dve.wait_ge(xhatT_filled[k], B)
                    nc.vector.memset(gated_identity, 0.0).then_inc(gated_identity_zeroed, 1)
                if n == AT_IDENTITY[1]:
                    dve.wait_ge(gated_identity_zeroed, 1)
                    for k in range(KD):
                        last = nc.vector.tensor_scalar(gated_identity[:, k, P * k:P * (k + 1)],
                                                       identity[:], gates[:, 1:2], None, ALU.mult)
                    last.then_inc(gated_identity_ready, 1)

            def copy_expert(e):
                dve.wait_ge(expertT_filled, e + 1)
                if e == 0:
                    dve.wait_ge(gated_identity_ready, 1)
                nc.vector.scalar_tensor_tensor(
                    expertT[:, :, e, :], misc_ps[:, EXPERT_BANK[e], :].rearrange("p (k f) -> p k f", k=KD),
                    gates[:, 1:2], gated_identity, ALU.mult, ALU.add).then_inc(expertT_copied, 1)

            def iteration(b, first=False, ln=True, prep=True):
                for n in range(TILES):
                    if prep:
                        prepare(b + 1, n)
                    else:
                        gate_identity(n)
                        if n in AT_EXPERT:
                            copy_expert(AT_EXPERT.index(n))
                    if not first:
                        finish(b - 1, n)
                    if ln:
                        layernorm(b + 2, n)
                    if first and n == 21:
                        scale_wo()
                    if n % PAIRS == AT_Z and not (first and n < Z_LAG * PAIRS):
                        invert_z(b, n // PAIRS - Z_LAG)
                    maxes(b, n)

            zero_stack(0)
            prepare(0, AT_CTX[1])
            for n in range(TILES):
                layernorm(0, n)
            normalise_first()
            split_lo(0, 0)
            split_lo(0, 1)
            prepare(0, AT_XHAT[1])
            split_lo(0, 2)
            split_lo(0, 3)
            centre_gate()
            zero_stack(1)
            for n in range(TILES):
                layernorm(1, n)
            dve.wait_ge(v_zeroed, 1)
            dve.wait_ge(wv_loaded, 48)
            for i in range(2):
                for s in range(2):
                    copy_v(0, i, s)
            dve.wait_ge(v_zeroed, 2)
            dve.wait_ge(gateT_zeroed, 1)
            dve.wait_ge(consts_ready, 2)
            iteration(0, first=True)
            with dve.Fori(1, B - 2) as b:
                iteration(b)
            iteration(B - 2, ln=False)
            iteration(B - 1, ln=False, prep=False)
            for blk in range(-Z_LAG, 0):
                invert_z(B, blk)

            steps = [0]

            def then(instruction):
                steps[0] += 1
                instruction.then_inc(plan, 1)
                dve.wait_ge(plan, steps[0])

            def add_up_tiles():
                then(nc.vector.tensor_tensor(tiles_upto[:],
                                             tiles_of[:].unsqueeze(1).to_broadcast([1, E, E]),
                                             upto[:], ALU.mult))
                then(nc.vector.reduce_sum(ends[:], tiles_upto[:], AX_X))

            def find_experts(n, weights):
                def over_tiles(v):
                    return v.unsqueeze(1).to_broadcast([1, n, E])

                then(nc.vector.tensor_tensor(ended[:, 0:n], tile_no[:, 0:n], over_tiles(ends[:]),
                                             ALU.is_ge))
                nc.vector.tensor_tensor(ended_tiles[:, 0:n], ended[:, 0:n], over_tiles(weights[:]),
                                        ALU.mult)
                then(nc.vector.reduce_sum(expert_f[:, 0:n], ended[:, 0:n], AX_X))
                then(nc.vector.reduce_sum(first_tile[:, 0:n], ended_tiles[:, 0:n], AX_X))

            def find_rows(first, n, offset):
                then(nc.vector.scalar_tensor_tensor(in_region[:, 0:n], tile_no[:, 0:n, 0], offset,
                                                    first_tile[:, 0:n], ALU.add, ALU.subtract))
                then(nc.vector.scalar_tensor_tensor(in_region[:, 0:n], expert_f[:, 0:n], float(E),
                                                    in_region[:, 0:n], ALU.is_lt, ALU.mult))
                then(nc.vector.scalar_tensor_tensor(row_f[:, 0:n], expert_f[:, 0:n],
                                                    float(REGION // P), in_region[:, 0:n],
                                                    ALU.mult, ALU.add))
                nc.vector.tensor_scalar(tile_expert[:, first:first + n], expert_f[:, 0:n], float(E - 1),
                                        None, ALU.min)
                nc.vector.tensor_scalar(tile_row[:, first:first + n], row_f[:, 0:n], float(P), None,
                                        ALU.mult).then_inc(plan_ready, 1)

            def plan_early():
                dve.wait_ge(counts_filled, 1)
                counts = misc_ps[0:1, 0, 0:E]
                then(nc.vector.scalar_tensor_tensor(past[:], counts.unsqueeze(2).to_broadcast([1, E, NT]),
                                                    float(1 - P), thresholds[:], ALU.add, ALU.is_gt))
                then(nc.vector.reduce_sum(tiles_of[:], past[:], AX_X))
                add_up_tiles()
                find_experts(EARLY, tiles_of)
                find_rows(0, EARLY, 0.0)
                nc.vector.memset(used[:, E:], 0.0)
                then(nc.vector.tensor_tensor(used[:, 0:E], tiles_of[:], ends[:], ALU.subtract))
                then(nc.vector.tensor_scalar(used[:, 0:E], used[:, 0:E], float(EARLY), 0.0, ALU.add,
                                             ALU.max))
                then(nc.vector.tensor_tensor(used[:, 0:E], used[:, 0:E], tiles_of[:], ALU.min))
                then(nc.vector.tensor_tensor(drop[:], used[:, 0:E], used[:, 1:], ALU.subtract))

            def count_late():
                dve.wait_ge(counts_filled, 2)
                counts = attn_ps[0:1, 1, 0:E]
                nc.vector.tensor_tensor(pad_row[:], counts, region_base[0:1, 0, :], ALU.add)\
                    .then_inc(plan_ready, 1)
                then(nc.vector.tensor_tensor(past[:], counts.unsqueeze(2).to_broadcast([1, E, NT]),
                                             thresholds[:], ALU.is_gt))
                then(nc.vector.reduce_sum(tiles_of[:], past[:], AX_X))
                then(nc.vector.tensor_tensor(tiles_of[:], tiles_of[:], used[:, 0:E], ALU.subtract))

            def add_rows(k):
                dve.wait_ge(expert_filled, k + 1)
                nc.vector.tensor_tensor(rows_in[:, k % SLOTS, 0:D], rows_in[:, k % SLOTS, 0:D],
                                        expert_banks[k % 2], ALU.add).then_inc(expert_read, 1)

            for what in ENDING:
                if what == "out":
                    plan_early()
                    for n in range(AT_X1_STATS[0]):
                        finish(B - 1, n)
                if what == "x1T":
                    for n in range(AT_X1_STATS[0], AT_LOGITS):
                        finish(B - 1, n)
                if what == "logits":
                    for n in range(AT_LOGITS, AT_RANK):
                        finish(B - 1, n)
                if what == "ranks":
                    for n in range(AT_RANK, TILES):
                        finish(B - 1, n)
                if what == "counts":
                    count_late()
                if what == "sums":
                    add_up_tiles()
                    then(nc.vector.tensor_tensor(drop[:], drop[:], tiles_of[:], ALU.add))
                if what == "experts":
                    find_experts(LATE, drop)
                if what == "rows":
                    find_rows(EARLY, LATE, used[:, 0:1])
                if isinstance(what, int):
                    add_rows(what)


_INS = ["x", "ctx_1024", "g_xattn", "g_ffn", "L0_xattn_w_q", "L0_xattn_b_q", "L0_xattn_w_k",
        "L0_xattn_b_k", "L0_xattn_w_v", "L0_xattn_b_v", "L0_xattn_w_o", "L0_xattn_b_o",
        "L0_ffn_gate_w", "L0_ffn_expert_w"]


def kernel(**inputs):
    import numpy as _np
    import concourse.bacc as _bacc
    from concourse import mybir as _mybir
    from concourse.bass_utils import run_bass_kernel_spmd as _run

    nc = _bacc.Bacc("TRN2", target_bir_lowering=False, num_devices=1)
    arrays, args = {}, []
    for name in _INS:
        a = _np.ascontiguousarray(inputs[name])
        arrays[f"in_{name}"] = a
        args.append(nc.dram_tensor(f"in_{name}", a.shape, _mybir.dt.from_np(a.dtype),
                                   kind="ExternalInput").ap())
    shape = tuple(inputs["x"].shape)
    args.append(nc.dram_tensor("out_x", shape, _mybir.dt.float32, kind="ExternalOutput").ap())
    attention_moe_kernel(nc, *args)
    r = _run(nc, [arrays], core_ids=[0])
    return r.results[0]["out_x"]
```
